# Optimizing a Trainium2 kernel written in Bass

```python
import numpy as np
import jax
import jax.numpy as jnp

def _softmax(x, axis=-1):
    return jax.nn.softmax(x, axis=axis)

def _gelu(x):
    return jax.nn.gelu(x, approximate=True)

def _silu(x):
    return jax.nn.silu(x)

def _sigmoid(x):
    return jax.nn.sigmoid(x)

def _layernorm(x, axis=-1, eps=1e-05):
    m = jnp.mean(x, axis=axis, keepdims=True)
    v = jnp.var(x, axis=axis, keepdims=True)
    return (x - m) / jnp.sqrt(v + eps)

def _scatter_add(tgt, idx, src, axis=0):
    return tgt.at[idx].add(src)

def _segment_sum(src, seg, n):
    return jax.ops.segment_sum(src, seg, n)
kernel_name = 'mk_seq_preln_d1_jaxref_r8_e08e81'

def setup_inputs(seed: int=0):
    np.random.seed(seed)
    _w = jnp.asarray

    def _L0_attn_setup():
        import jax, jax.numpy as jnp
        import numpy as np
        B, S, D = (2, 256, 128)
        H = 16
        K = 21
        HD = D // H

        def _tisa_bias(amplitudes, sharpness, offsets, seq_len):
            rel = jnp.arange(-(seq_len - 1), seq_len, dtype=jnp.float32)
            d = rel[None, None, :] - offsets[:, :, None]
            scores = amplitudes[:, :, None] * jnp.exp(-jnp.abs(sharpness)[:, :, None] * d * d)
            scores = scores.sum(axis=1)
            idx = jnp.arange(seq_len)
            rel_idx = idx[None, :] - idx[:, None] + (seq_len - 1)
            return scores[:, rel_idx]
        key = jax.random.key(seed)
        ks = jax.random.split(key, 7)
        x = jax.random.normal(ks[0], (B, S, D), dtype=jnp.float32)
        w_in = jax.random.normal(ks[1], (D, 3 * D), dtype=jnp.float32) * (1.0 / np.sqrt(D))
        w_gate = jax.random.normal(ks[2], (D, 2 * D), dtype=jnp.float32) * (1.0 / np.sqrt(D))
        b_gate = jnp.zeros((2 * D,), dtype=jnp.float32)
        amplitudes = jax.random.normal(ks[3], (H, K), dtype=jnp.float32) * 0.1
        sharpness = jax.random.uniform(ks[4], (H, K), dtype=jnp.float32, minval=0.05, maxval=0.3)
        max_fv, min_fv = (S // 2, 5)
        offsets = jax.random.uniform(ks[5], (H, K), dtype=jnp.float32, minval=-float(max_fv), maxval=float(max_fv))
        return {'x': x, 'w_in': w_in, 'w_gate': w_gate, 'b_gate': b_gate, 'amplitudes': amplitudes, 'sharpness': sharpness, 'offsets': offsets}
    _L0_attn_in = _L0_attn_setup()

    def _L0_ffn_setup():
        import jax, jax.numpy as jnp
        import numpy as np
        FP8_MAX = 448.0

        def quant_fp8(x):
            amax = jnp.max(jnp.abs(x)).astype(jnp.float32)
            scale = jnp.minimum(FP8_MAX / jnp.maximum(amax, 1e-12), FP8_MAX)
            x_fp8 = jnp.clip(x * scale, -FP8_MAX, FP8_MAX).astype(jnp.float8_e4m3fn)
            return (x_fp8, 1.0 / scale)
        key = jax.random.key(seed)
        k1, k2, k3 = jax.random.split(key, 3)
        B, S, IN, OUT = (4, 1024, 128, 128)
        input = jax.random.normal(k1, (B, S, IN), dtype=jnp.float32)
        bound = 1.0 / np.sqrt(IN)
        weight = jax.random.uniform(k2, (OUT, IN), dtype=jnp.float32, minval=-bound, maxval=bound)
        bias = jax.random.uniform(k3, (OUT,), dtype=jnp.float32, minval=-bound, maxval=bound)
        return {'input': input, 'weight': weight, 'bias': bias}
    _L0_ffn_in = _L0_ffn_setup()
    _d = {'L0_attn_x': _L0_attn_in['x'], 'L0_attn_w_in': _L0_attn_in['w_in'], 'L0_attn_w_gate': _L0_attn_in['w_gate'], 'L0_attn_b_gate': _L0_attn_in['b_gate'], 'L0_attn_amplitudes': _L0_attn_in['amplitudes'], 'L0_attn_sharpness': _L0_attn_in['sharpness'], 'L0_attn_offsets': _L0_attn_in['offsets'], 'L0_ffn_weight': _L0_ffn_in['weight'], 'L0_ffn_bias': _L0_ffn_in['bias']}
    _x0 = _d['L0_attn_x']
    _d['L0_attn_x'] = jax.random.normal(jax.random.fold_in(jax.random.key(seed), 1), (4, 1024, 128), dtype=_x0.dtype)
    del _x0
    return _d

def reference(L0_attn_x, L0_attn_w_in, L0_attn_w_gate, L0_attn_b_gate, L0_attn_amplitudes, L0_attn_sharpness, L0_attn_offsets, L0_ffn_weight, L0_ffn_bias):

    def _L0_attn_ref(x, w_in, w_gate, b_gate, amplitudes, sharpness, offsets):
        import jax, jax.numpy as jnp
        import numpy as np
        B, S, D = (2, 256, 128)
        H = 16
        K = 21
        HD = D // H

        def _tisa_bias(amplitudes, sharpness, offsets, seq_len):
            rel = jnp.arange(-(seq_len - 1), seq_len, dtype=jnp.float32)
            d = rel[None, None, :] - offsets[:, :, None]
            scores = amplitudes[:, :, None] * jnp.exp(-jnp.abs(sharpness)[:, :, None] * d * d)
            scores = scores.sum(axis=1)
            idx = jnp.arange(seq_len)
            rel_idx = idx[None, :] - idx[:, None] + (seq_len - 1)
            return scores[:, rel_idx]
        b, s, d = x.shape
        proj = x @ w_in
        k, v, q = jnp.split(proj, 3, axis=-1)

        def heads(t):
            return t.reshape(b, s, H, HD).transpose(0, 2, 1, 3)
        q, k, v = (heads(q), heads(k), heads(v))
        scale = 1.0 / jnp.sqrt(jnp.float32(HD))
        scores = jnp.einsum('bhqd,bhkd->bhqk', q, k) * scale
        scores = scores + _tisa_bias(amplitudes, sharpness, offsets, s)[None]
        weights = jax.nn.softmax(scores, axis=-1)
        attn = jnp.einsum('bhqk,bhkd->bhqd', weights, v)
        out = attn.transpose(0, 2, 1, 3).reshape(b, s, d)
        gated = out @ w_gate + b_gate
        a, g = jnp.split(gated, 2, axis=-1)
        return a * jax.nn.sigmoid(g)

    def _L0_ffn_ref(input, weight, bias):
        import jax, jax.numpy as jnp
        import numpy as np
        FP8_MAX = 448.0

        def quant_fp8(x):
            amax = jnp.max(jnp.abs(x)).astype(jnp.float32)
            scale = jnp.minimum(FP8_MAX / jnp.maximum(amax, 1e-12), FP8_MAX)
            x_fp8 = jnp.clip(x * scale, -FP8_MAX, FP8_MAX).astype(jnp.float8_e4m3fn)
            return (x_fp8, 1.0 / scale)
        prev_shape = input.shape
        x2d = input.reshape(-1, weight.shape[1])
        w_fp8, w_scale = quant_fp8(weight)
        x_fp8, x_scale = quant_fp8(x2d)
        acc = jnp.matmul(x_fp8.astype(jnp.float32), w_fp8.astype(jnp.float32).T)
        out2d = (acc * (x_scale * w_scale) + bias).astype(jnp.bfloat16)
        out = out2d.reshape(*prev_shape[:-1], weight.shape[0]).astype(input.dtype)
        return out
    x = L0_attn_x
    x = x + _L0_attn_ref(_layernorm(x, axis=-1), L0_attn_w_in, L0_attn_w_gate, L0_attn_b_gate, L0_attn_amplitudes, L0_attn_sharpness, L0_attn_offsets)
    x = x + _L0_ffn_ref(_layernorm(x, axis=-1), L0_ffn_weight, L0_ffn_bias)
    return x

_drawn_inputs = setup_inputs


def setup_inputs(seed=0):
    import zlib

    import numpy as np

    out = dict(_drawn_inputs(seed))
    spreads = {'L0_attn_b_gate': (0.0, 0.1)}
    factors = {'L0_attn_amplitudes': 64.0, 'L0_attn_sharpness': 64.0, 'L0_attn_offsets': 64.0}
    for name, (base, spread) in spreads.items():
        noise = np.random.default_rng([zlib.crc32(name.encode()), seed]).standard_normal(out[name].shape)
        drawn = base * np.exp(spread * noise) if base else spread * noise
        out[name] = jnp.asarray(drawn.astype(out[name].dtype))
    for name, factor in factors.items():
        out[name] = (out[name] * factor).astype(out[name].dtype)
    return out
```

```python
from contextlib import ExitStack

import concourse.bass as bass
from concourse import mybir

F32 = mybir.dt.float32
F16 = mybir.dt.float16
BF16 = mybir.dt.bfloat16
I32 = mybir.dt.int32
ALU = mybir.AluOpType
ACT = mybir.ActivationFunctionType
AX = mybir.AxisListType

B, S, D = 4, 1024, 128
H, KB = 16, 21
HD = D // H
P = 128
NTOK = B * S
NT = NTOK // P
TB = S // P
HALF = 512
PAIRS = H * KB
PG = 3
PP = PAIRS // PG
GN = 2 * S
T128W = 2 * S - P
T64W = 2 * S - 64
NH2 = H // 2
VW = 32
EPS = 1e-5
QSCALE = float(HD) ** -0.5
SAFE = 60.0
FP8_MAX = 448.0
DPG = 3
SETS = 4
LAG = 2
DPH = DPG * TB


def attention_block(nc, io, out):
    with ExitStack() as ctx:
        def sb(name, shape, dt):
            return ctx.enter_context(nc.sbuf_tensor(name, shape, dt))

        def sem(name):
            return ctx.enter_context(nc.semaphore(name))

        def dram(name, shape, dt):
            return nc.dram_tensor(name, shape, dt, kind="Internal").ap()

        q_dram = dram("q_scratch", [2, P, NTOK], F16)
        k_dram = dram("k_scratch", [2, P, NTOK], F16)
        g_dram = dram("g_scratch", [32, GN], F32)
        gh_dram = dram("gh_scratch", [32, GN], F16)
        gl_dram = dram("gl_scratch", [32, GN], F16)
        m_dram = dram("m_scratch", [H, NTOK], F16)
        o_dram = dram("o_scratch", [B, H, HD + 1, S], F32)
        bg_dram = dram("bg_scratch", [3, 2 * D], BF16)

        x_sb = sb("x_sb", [P, NT, D], F32)
        ident = sb("ident", [P, P], F32)
        win = sb("win", [P, 3 * D], F32)
        wgate = sb("wgate", [P, 2 * D], F32)
        wffn = sb("wffn", [P, D], F32)
        ffn_bias = sb("ffn_bias", [P, D], F32)
        bgate = sb("bgate", [1, 2 * D], F32)
        bg_parts = sb("bg_parts", [1, 3, 2 * D], BF16)
        bg_rows = sb("bg_rows", [3, 2 * D], BF16)
        ones_row = sb("ones_row", [1, P], F32)
        bg_ones = sb("bg_ones", [3, P], BF16)
        ident2 = sb("ident2", [P, 64], F16)
        v_all = sb("v_all", [P, NT, D], F32)
        stats = sb("stats", [P, NT, 6], F32)
        st = sb("st", [P, 8, NT], F32)
        flag = sb("flag", [1, 1], I32)
        small = sb("small", [P, 32], F32)
        qb = [sb(f"qb{p}", [P, NTOK], F16) for p in range(2)]
        kb = [sb(f"kb{p}", [P, NTOK], F16) for p in range(2)]
        t64s = sb("t64s", [P, 2, 2 * S], F16)
        t64 = [t64s[:, p, :] for p in range(2)]
        t128 = [sb(f"t128_{p}", [P, 2 * S], F32) for p in range(2)]
        vst = [sb(f"vst{p}", [P, NT, VW], F32) for p in range(2)]
        pbuf = sb("pbuf", [P, 8, S], F32)
        o_sbs = sb("o_sbs", [P, 2, S], F32)
        o_sb = [o_sbs[:, p, :] for p in range(2)]
        big = pbuf[:, :, :].rearrange("p a c -> p (a c)")
        xn = big[:, 0:NTOK].rearrange("p (n d) -> p n d", d=D)
        xT = big[:, NTOK:2 * NTOK]
        split = sb("split", [P, 4, NTOK], F16)
        splitf = split[:, :, :].rearrange("p a c -> p (a c)").bitcast(F32)
        gauss = [t128[0][0:PP, :], t128[1][0:PP, :], o_sbs[0:PP, :, :].rearrange("p a c -> p (a c)")]
        ps = ctx.enter_context(nc.psum_tensor("ps", [P, 8, HALF], F32))

        def banks(a, n):
            return ps[:, a:a + n, :].rearrange("p a c -> p (a c)")

        amp = sb("amp", [PP, PG], F32)
        shp = sb("shp", [PP, PG], F32)
        off = sb("off", [PP, PG], F32)
        nshp = sb("nshp", [PP, PG], F32)
        sel = sb("sel", [PP, PG, 32], F32)
        rel = t64s[0:PP, :, :].rearrange("p a c -> p (a c)").bitcast(F32)
        zeros = sb("zeros", [P, HALF], F16)
        hsel = sb("hsel", [P, 32], F32)
        hselb = sb("hselb", [P, 32], BF16)
        sq = [xn[:, b * TB:(b + 1) * TB, :].rearrange("p n d -> p (n d)").bitcast(BF16)
              .rearrange("p (i c) -> p i c", i=2) for b in range(B)]
        gv = sb("gv", [P, HALF], F32)
        gvh = sb("gvh", [P, HALF], F16)
        gvl = sb("gvl", [P, HALF], F16)
        bnd = sb("bnd", [P, 4], F32)
        bndr = sb("bndr", [4, 1], F32)
        bndt = sb("bndt", [1, 4], F32)
        dve_done = sem("dve_done")
        dve_count = [0]

        def chain(eng, ins):
            dve_count[0] += 1
            ins.then_inc(dve_done, 1)
            eng.wait_ge(dve_done, dve_count[0])

        x_in = [sem(f"x_in{b}") for b in range(B)]
        consts_in = sem("consts_in")
        win_in = sem("win_in")
        gauss_in = sem("gauss_in")
        var_ready = sem("var_ready")
        std_ready = sem("std_ready")
        xn_ready = sem("xn_ready")
        xnT_ready = sem("xnT_ready")
        xT_ready = sem("xT_ready")
        q_ready = sem("q_ready")
        k_ready = sem("k_ready")
        v_ready = sem("v_ready")
        qh_ready = sem("qh_ready")
        kh_ready = sem("kh_ready")
        v_copied = sem("v_copied")
        ql_ready = sem("ql_ready")
        kl_ready = sem("kl_ready")
        sq_ready = sem("sq_ready")
        norm_ready = sem("norm_ready")
        arg_ready = sem("arg_ready")
        exp_ready = sem("exp_ready")
        amp_ready = sem("amp_ready")
        gsum_ready = sem("gsum_ready")
        gh_ready = sem("gh_ready")
        gl_ready = sem("gl_ready")
        bnd_ready = sem("bnd_ready")
        bndT_ready = sem("bndT_ready")
        bndr_ready = sem("bndr_ready")
        bndt_ready = sem("bndt_ready")
        scratch_out = sem("scratch_out")
        zeros_ready = sem("zeros_ready")
        hsel_ready = sem("hsel_ready")
        bg_ready = sem("bg_ready")
        n_out = [0]
        groups_done = sem("groups_done")
        o_ready = sem("o_ready")
        o_stored = [sem(f"o_stored{p}") for p in range(2)]
        g_row = sem("g_row")
        g_stored = sem("g_stored")

        def moments(eng, t, done):
            me, mo = stats[:, t, 1], stats[:, t, 4]
            ve, vo = stats[:, t, 2], stats[:, t, 5]
            chain(eng, eng.tensor_tensor(st[:, 4, t], me, mo, ALU.add))
            chain(eng, eng.tensor_scalar(st[:, 0, t], st[:, 4, t], 0.5, None, ALU.mult))
            chain(eng, eng.tensor_tensor(st[:, 4, t], me, mo, ALU.subtract))
            chain(eng, eng.scalar_tensor_tensor(out=st[:, 4, t], in0=st[:, 4, t], scalar=0.25,
                                                in1=st[:, 4, t], op0=ALU.mult, op1=ALU.mult))
            chain(eng, eng.tensor_tensor(st[:, 5, t], ve, vo, ALU.add))
            chain(eng, eng.scalar_tensor_tensor(out=st[:, 1, t], in0=st[:, 5, t], scalar=1.0 / D,
                                                in1=st[:, 4, t], op0=ALU.mult, op1=ALU.add))
            chain(eng, eng.tensor_scalar(st[:, 1, t], st[:, 1, t], EPS, None, ALU.add))
            eng.tensor_copy(st[:, 6, t], st[:, 1, t]).then_inc(done, 1)

        x_t = io["x"].rearrange("b (n p) d -> p (b n) d", p=P)

        with nc.Block() as block:
            @block.sync
            def _(eng):
                for b in range(B):
                    eng.dma_start(x_sb[:, b * TB:(b + 1) * TB, :], x_t[:, b * TB:(b + 1) * TB, :])\
                       .then_inc(x_in[b], 16)
                eng.dma_start(wffn[:, :], io["w_ffn"]).then_inc(consts_in, 16)
                eng.dma_start(wgate[:, :], io["w_gate"]).then_inc(consts_in, 16)
                eng.dma_start(bgate[:, :], io["b_gate"].rearrange("(a n) -> a n", a=1)).then_inc(consts_in, 16)
                eng.dma_start(ffn_bias[:, :], bass.AP(tensor=io["ffn_bias"].tensor, offset=0,
                                                      ap=[[0, P], [1, D]])).then_inc(consts_in, 16)
                for b in range(B):
                    cols = slice(b * S, (b + 1) * S)
                    for ready, part, dst, hl in ((qh_ready, 0, q_dram, 0), (kh_ready, 2, k_dram, 0),
                                                 (ql_ready, 1, q_dram, 1), (kl_ready, 3, k_dram, 1)):
                        eng.wait_ge(ready, b + 1)
                        eng.dma_start(dst[hl, :, cols], split[:, part, cols]).then_inc(scratch_out, 16)
                        n_out[0] += 1
                eng.wait_ge(gh_ready, 1)
                eng.wait_ge(gl_ready, 2)
                for src, dst in ((gv, g_dram), (gvh, gh_dram), (gvl, gl_dram)):
                    for c in range(4):
                        eng.dma_start(dst[:, c * HALF:(c + 1) * HALF], src[32 * c:32 * c + 32, :])\
                           .then_inc(scratch_out, 16)
                        n_out[0] += 1
                eng.wait_ge(zeros_ready, 1)
                eng.dma_start(m_dram.rearrange("h (a c) -> (h a) c", c=HALF), zeros[:, :])\
                   .then_inc(scratch_out, 16)
                eng.wait_ge(bg_ready, 1)
                eng.dma_start(bg_dram.rearrange("(o a) c -> o a c", o=1), bg_parts[:, :, :])\
                   .then_inc(scratch_out, 16)
                n_out[0] += 2
                eng.wait_ge(scratch_out, 16 * n_out[0])
                eng.dma_start(bg_rows[:, :], bg_dram).then_inc(scratch_out, 16)
                eng.wait_ge(scratch_out, 16 * n_out[0] + 16)

            @block.gpsimd
            def _(eng):
                eng.memset(zeros[:, :], 0.0).then_inc(zeros_ready, 1)
                fills = []
                for p in range(2):
                    for t in (qb[p], kb[p]):
                        fills.append((t[32:64, :].bitcast(F32), 0.0))
                        fills.append((t[64:P, :].bitcast(F32), 0.0))
                    fills.append((kb[p][32:33, :], -1.0))
                    fills.append((vst[p][:, :, :], 0.0))
                    fills.append((vst[p][:, :, HD:HD + 1], 1.0))
                for n, (dst, value) in enumerate(fills):
                    eng.wait_ge(zeros_ready, n + 1)
                    eng.memset(dst, value).then_inc(zeros_ready, 1)
                eng.wait_ge(zeros_ready, len(fills) + 1)
                eng.memset(bg_ones[:, :], 1.0).then_inc(groups_done, SETS)
                eng.wait_ge(groups_done, SETS)
                eng.memset(ones_row[:, :], 1.0).then_inc(o_stored[1], 16 * B)
                eng.sem_inc(o_stored[0], 16 * B)
                eng.sem_inc(o_ready, 1)
                eng.sem_inc(g_row, 1)
                eng.sem_inc(g_stored, 16)

            @block.scalar
            def _(eng):
                with nc.allow_non_contiguous_dma(reason="336 parameters"):
                    for dst, name in ((amp, "amplitudes"), (shp, "sharpness"), (off, "offsets")):
                        eng.dma_start(dst[:, :], io[name].rearrange("h k -> (h k)")
                                      .rearrange("(g p) -> p g", p=PP)).then_inc(gauss_in, 16)
                eng.dma_start(win[:, :], io["w_in"]).then_inc(win_in, 16)
                eng.dma_start(ident[:, :], io["c_ident"]).then_inc(win_in, 16)
                eng.dma_start(sel[:, :, :], io["c_sel"]).then_inc(gauss_in, 16)
                eng.dma_start(rel, bass.AP(tensor=io["c_rel"].tensor, offset=0,
                                                 ap=[[0, PP], [1, GN]])).then_inc(gauss_in, 16)
                eng.dma_start(ident2[:, :], io["c_ident2"]).then_inc(win_in, 16)
                eng.dma_start(hsel[:, :], io["c_hsel"]).then_inc(win_in, 16)
                for b in range(B):
                    eng.wait_ge(var_ready, b + 1)
                    eng.activation(st[:, 2, b * TB:(b + 1) * TB], st[:, 1, b * TB:(b + 1) * TB], ACT.Sqrt)\
                       .then_inc(std_ready, 1)
                for g in range(PG):
                    eng.wait_ge(arg_ready, g + 1)
                    eng.activation(gauss[g], gauss[g], ACT.Exp).then_inc(exp_ready, 1)
                for b in range(B):
                    cols = slice(b * S, (b + 1) * S)
                    back = slice(S - 1 + b * S, b * S - 1 if b else None, -1)
                    eng.wait_ge(q_ready, b + 1)
                    eng.activation(split[:, 0, back], banks(2, 2), ACT.Copy, scale=QSCALE)\
                       .then_inc(qh_ready, 1)
                    eng.activation(sq[b][:, 0, :], banks(2, 2), ACT.Square, scale=QSCALE)\
                       .then_inc(sq_ready, 1)
                    eng.wait_ge(k_ready, b + 1)
                    eng.activation(split[:, 2, cols], banks(4, 2), ACT.Copy).then_inc(kh_ready, 1)
                    eng.activation(sq[b][:, 1, :], banks(4, 2), ACT.Square).then_inc(sq_ready, 1)
                    eng.wait_ge(v_ready, b + 1)
                    eng.activation(v_all[:, b * TB:(b + 1) * TB, :].rearrange("p n d -> p (n d)"),
                                   banks(6, 2), ACT.Copy).then_inc(v_copied, 1)

            @block.vector
            def _(eng):
                eng.wait_ge(gauss_in, 80)
                chain(eng, eng.tensor_scalar(nshp[:, :], shp[:, :], -1.0, None, ALU.mult))
                chain(eng, eng.tensor_tensor(nshp[:, :], nshp[:, :], shp[:, :], ALU.min))
                for g in range(PG):
                    last = eng.tensor_scalar(sel[:, g, :], sel[:, g, :], amp[:, g:g + 1], None, ALU.mult)
                last.then_inc(amp_ready, 1)
                for b in range(B):
                    t = slice(b * TB, (b + 1) * TB)
                    eng.wait_ge(x_in[b], 16)
                    for n in range(b * TB, (b + 1) * TB):
                        last = eng.bn_stats(stats[:, n, :], x_sb[:, n, :])
                    chain(eng, last)
                    moments(eng, t, var_ready)
                    eng.wait_ge(std_ready, b + 1)
                    chain(eng, eng.reciprocal(st[:, 3, t], st[:, 2, t]))
                    for n in range(b * TB, (b + 1) * TB):
                        last = eng.tensor_scalar(xn[:, n, :], x_sb[:, n, :], st[:, 0, n:n + 1],
                                                 st[:, 3, n:n + 1], ALU.subtract, ALU.mult)
                    last.then_inc(xn_ready, 1)
                for g in range(PG):
                    chain(eng, eng.tensor_scalar(gauss[g], rel, off[:, g:g + 1], None,
                                                 ALU.subtract))
                    eng.scalar_tensor_tensor(out=gauss[g], in0=gauss[g],
                                             scalar=nshp[:, g:g + 1], in1=gauss[g],
                                             op0=ALU.mult, op1=ALU.mult).then_inc(arg_ready, 1)
                    if g == 0:
                        eng.wait_ge(win_in, 64)
                        eng.tensor_copy(hselb[:, :], hsel[:, :]).then_inc(hsel_ready, 1)
                for b in range(B):
                    cols = slice(b * S, (b + 1) * S)
                    back = slice(S - 1 + b * S, b * S - 1 if b else None, -1)
                    eng.wait_ge(xnT_ready, b + 1)
                    eng.tensor_copy(xT[:, cols], banks(0, 2)).then_inc(xT_ready, 1)
                    eng.wait_ge(sq_ready, 2 * b + 1)
                    eng.scalar_tensor_tensor(out=split[:, 1, back], in0=banks(2, 2), scalar=QSCALE,
                                             in1=split[:, 0, back], op0=ALU.mult, op1=ALU.subtract)\
                       .then_inc(ql_ready, 1)
                    eng.wait_ge(sq_ready, 2 * b + 2)
                    eng.tensor_tensor(split[:, 3, cols], banks(4, 2), split[:, 2, cols], ALU.subtract)\
                       .then_inc(kl_ready, 1)
                eng.wait_ge(consts_in, 64)
                chain(eng, eng.tensor_copy(bg_parts[:, 0, :], bgate[:, :]))
                chain(eng, eng.tensor_tensor(bgate[:, :], bgate[:, :], bg_parts[:, 0, :], ALU.subtract))
                chain(eng, eng.tensor_copy(bg_parts[:, 1, :], bgate[:, :]))
                chain(eng, eng.tensor_tensor(bgate[:, :], bgate[:, :], bg_parts[:, 1, :], ALU.subtract))
                eng.tensor_copy(bg_parts[:, 2, :], bgate[:, :]).then_inc(bg_ready, 1)
                eng.wait_ge(gsum_ready, 1)
                chain(eng, eng.tensor_copy(gvh[:, :], ps[:, 0, :]))
                eng.tensor_copy(gv[:, :], ps[:, 0, :]).then_inc(gh_ready, 1)
                eng.tensor_tensor(gvl[:, :], ps[:, 0, :], gvh[:, :], ALU.subtract).then_inc(gl_ready, 1)
                eng.tensor_reduce(bnd[:, 2:3], ps[:, 0, :], AX.X, ALU.max, apply_absolute_value=True)\
                   .then_inc(gl_ready, 1)
                eng.wait_ge(norm_ready, 1)
                eng.tensor_reduce(bnd[:, 0:1], banks(4, 2), AX.X, ALU.max)
                eng.tensor_reduce(bnd[:, 1:2], banks(6, 2), AX.X, ALU.max).then_inc(bnd_ready, 1)
                eng.wait_ge(bndT_ready, 1)
                eng.tensor_reduce(bndr[0:3, :], ps[0:3, 3, 0:P], AX.X, ALU.max).then_inc(bndr_ready, 1)
                eng.wait_ge(bndt_ready, 1)
                chain(eng, eng.tensor_copy(bndt[:, 0:3], ps[0:1, 4, 0:3]))
                chain(eng, eng.scalar_tensor_tensor(out=small[0:1, 0:1], in0=bndt[:, 0:1], scalar=1.05,
                                                    in1=bndt[:, 1:2], op0=ALU.mult, op1=ALU.mult))
                chain(eng, eng.tensor_scalar(small[0:1, 1:2], bndt[:, 2:3], -1.0, SAFE, ALU.mult, ALU.add))
                chain(eng, eng.tensor_scalar(small[0:1, 1:2], small[0:1, 1:2], 0.0, None, ALU.max))
                chain(eng, eng.tensor_tensor(small[0:1, 2:3], small[0:1, 1:2], small[0:1, 1:2], ALU.mult))
                chain(eng, eng.tensor_tensor(small[0:1, 3:4], small[0:1, 0:1], small[0:1, 2:3], ALU.is_le))
                chain(eng, eng.tensor_scalar(flag[:, :], small[0:1, 3:4], -1.0, 1.0, ALU.mult, ALU.add))

            @block.tensor
            def _(eng):
                eng.wait_ge(win_in, 64)
                for b in range(B):
                    eng.wait_ge(xn_ready, b + 1)
                    if b >= 1:
                        eng.wait_ge(xT_ready, b)
                    for n in range(TB):
                        last = eng.transpose(banks(0, 2)[:, n * P:(n + 1) * P], xn[:, b * TB + n, :], ident[:, :])
                    last.then_inc(xnT_ready, 1)
                    eng.wait_ge(xT_ready, b + 1)
                    if b >= 1:
                        eng.wait_ge(ql_ready, b)
                        eng.wait_ge(sq_ready, 2 * b)
                    for c in range(2):
                        last = eng.matmul(ps[:, 2 + c, :], win[:, 2 * D:3 * D],
                                          xT[:, b * S + c * HALF:b * S + (c + 1) * HALF], start=True, stop=True)
                    last.then_inc(q_ready, 1)
                    if b >= 1:
                        eng.wait_ge(kl_ready, b)
                    for c in range(2):
                        last = eng.matmul(ps[:, 4 + c, :], win[:, 0:D],
                                          xT[:, b * S + c * HALF:b * S + (c + 1) * HALF], start=True, stop=True)
                    last.then_inc(k_ready, 1)
                    if b >= 1:
                        eng.wait_ge(v_copied, b)
                    for n in range(TB):
                        last = eng.matmul(banks(6, 2)[:, n * P:(n + 1) * P],
                                          xT[:, b * S + n * P:b * S + (n + 1) * P], win[:, D:2 * D],
                                          start=True, stop=True)
                    last.then_inc(v_ready, 1)
                eng.wait_ge(amp_ready, 1)
                for g in range(PG):
                    eng.wait_ge(exp_ready, g + 1)
                    for c in range(4):
                        last = eng.matmul(ps[32 * c:32 * c + 32, 0, :], sel[:, g, :],
                                          gauss[g][:, c * HALF:(c + 1) * HALF],
                                          start=(g == 0), stop=(g == PG - 1))
                last.then_inc(gsum_ready, 1)
                eng.wait_ge(hsel_ready, 1)
                eng.wait_ge(sq_ready, 2 * B)
                eng.wait_ge(kl_ready, B)
                eng.wait_ge(v_copied, B)
                for i in range(2):
                    for c in range(2):
                        for b in range(B):
                            last = eng.matmul(ps[32 * b:32 * b + 32, 4 + 2 * i + c, :], hselb[:, :],
                                              sq[b][:, i, c * HALF:(c + 1) * HALF],
                                              start=True, stop=True)
                last.then_inc(norm_ready, 1)
                eng.wait_ge(bnd_ready, 1)
                eng.wait_ge(gl_ready, 2)
                eng.transpose(ps[0:3, 3, 0:P], bnd[:, 0:3], ident[:, :]).then_inc(bndT_ready, 1)
                eng.wait_ge(bndr_ready, 1)
                eng.transpose(ps[0:1, 4, 0:3], bndr[0:3, :], ident[0:3, 0:3]).then_inc(bndt_ready, 1)

        def slice_of(t, h, rows, width):
            v = t[h, :]
            return bass.AP(tensor=v.tensor, offset=v.offset, ap=[[1, rows], [1, width]])

        def load_head(eng, h, p, done):
            for rep in range(2):
                eng.dma_start(qb[p][16 * rep:16 * rep + 16, :],
                              q_dram.rearrange("a (h d) n -> h a d n", d=HD)[h]).then_inc(done, 16)
            for hl in range(2):
                for rep in range(2):
                    r = 16 * hl + 8 * rep
                    eng.dma_start(kb[p][r:r + 8, :],
                                  k_dram.rearrange("a (h d) n -> h a d n", d=HD)[h, hl]).then_inc(done, 16)
            eng.dma_start(t128[p][:, 0:T128W], slice_of(g_dram, h, P, T128W)).then_inc(done, 16)
        LOADS_G = 7

        m_sb = sb("m_sb", [P, NT], F32)
        m_row = sb("m_row", [NT, P], F16)
        g_loaded = sem("g_loaded")
        g_steps = sem("g_steps")
        g_scores = sem("g_scores")
        g_summed = sem("g_summed")
        g_max = sem("g_max")
        g_turned = sem("g_turned")
        zsum = [pbuf[:, i, :] for i in range(2)]

        with nc.Block() as block:
            @block.sync
            def _(eng):
                f = eng.value_load(flag[0:1, 0:1], min_val=0, max_val=1)
                with eng.If(f == 1):
                    with eng.Fori(0, H) as h:
                        eng.wait_ge(g_row, h + 1)
                        eng.sem_inc(g_steps, 1)
                        load_head(eng, h, 0, g_loaded)
                        eng.wait_ge(g_row, h + 2)
                        eng.sem_inc(g_steps, 1)
                        eng.dma_start(m_dram[h, :].rearrange("(n p) -> n p", p=P), m_row[:, :])\
                           .then_inc(g_stored, 16)
                        eng.wait_ge(g_stored, h * 16 + 32)
                        eng.sem_inc(g_steps, 1)

            @block.tensor
            def _(eng):
                f = eng.value_load(flag[0:1, 0:1], min_val=0, max_val=1)
                with eng.If(f == 1):
                    with eng.Fori(0, H) as h:
                        eng.wait_ge(g_loaded, h * (16 * LOADS_G) + 16 * LOADS_G)
                        for n in range(NT):
                            b = n // TB
                            if n >= 2:
                                eng.wait_ge(g_summed, h * NT + (n - 1))
                            for c in range(2):
                                last = eng.matmul(ps[:, 2 * (n % 2) + c, :], qb[0][0:32, n * P:(n + 1) * P],
                                                  kb[0][0:32, b * S + c * HALF:b * S + (c + 1) * HALF],
                                                  start=True, stop=True)
                            last.then_inc(g_scores, 1)
                        eng.wait_ge(g_max, h * NT + NT)
                        eng.transpose(ps[0:NT, 4, 0:P], m_sb[:, :], ident[:, :]).then_inc(g_turned, 1)

            @block.vector
            def _(eng):
                f = eng.value_load(flag[0:1, 0:1], min_val=0, max_val=1)
                with eng.If(f == 1):
                    with eng.Fori(0, H) as h:
                        for n in range(NT):
                            c0 = (n % TB) * P
                            eng.wait_ge(g_scores, h * NT + (n + 1))
                            eng.tensor_tensor(zsum[n % 2], banks(2 * (n % 2), 2), t128[0][:, c0:c0 + S],
                                              ALU.add).then_inc(g_summed, 1)
                            eng.wait_ge(g_summed, h * NT + (n + 1))
                            eng.tensor_reduce(m_sb[:, n:n + 1], zsum[n % 2], AX.X, ALU.max).then_inc(g_max, 1)
                        eng.wait_ge(g_turned, h + 1)
                        eng.wait_ge(g_stored, h * 16 + 16)
                        eng.tensor_copy(m_row[:, :], ps[0:NT, 4, 0:P]).then_inc(g_row, 1)

        queue_steps = sem("queue_steps")
        head_in = [sem(f"head_in{p}") for p in range(2)]
        vst_in = sem("vst_in")
        sd_ready = sem("sd_ready")
        sp_ready = sem("sp_ready")
        z_ready = sem("z_ready")
        p_ready = sem("p_ready")

        GPH = TB
        LOADS = LOADS_G + 3
        acc = banks(6, 2)

        def settled(eng, s, value):
            eng.wait_ge(s, value)
            eng.sem_inc(queue_steps, 1)

        def slot(g, b):
            n = 4 * (g % SETS) + b
            return pbuf[:, n, :] if n < 8 else splitf[:, (n - 8) * S:(n - 7) * S]

        def unit(k):
            return 2 * (k % 2)

        with nc.Block() as block:
            @block.sync
            def _(eng):
                def load(h, p):
                    if not isinstance(h, int):
                        h = nc.s_assert_within(h, 0, H - 1, skip_runtime_bounds_check_because="the branches around it keep it in range")
                    load_head(eng, h, p, head_in[p])
                    eng.dma_start(qb[p][32:33, :], m_dram[h, :].rearrange("(a n) -> a n", a=1))\
                       .then_inc(head_in[p], 16)
                    eng.dma_start(t64[p][0:64, 0:T64W], slice_of(gh_dram, h, 64, T64W)).then_inc(head_in[p], 16)
                    eng.dma_start(t64[p][64:P, 0:T64W], slice_of(gl_dram, h, 64, T64W)).then_inc(head_in[p], 16)

                def store(h, p):
                    if not isinstance(h, int):
                        h = nc.s_assert_within(h, 0, H - 1, skip_runtime_bounds_check_because="the branches around it keep it in range")
                    for b in range(B):
                        eng.dma_start(o_dram[b].rearrange("h r n -> h r n")[h],
                                      o_sb[p][32 * b:32 * b + HD + 1, :]).then_inc(o_stored[p], 16)

                load(0, 0)
                with eng.Fori(0, NH2) as i:
                    settled(eng, groups_done, i * (2 * GPH) + SETS)
                    load(i * 2 + 1, 1)
                    with eng.If(i > 0):
                        settled(eng, o_ready, i * 2 + 1)
                        store(i * 2 - 1, 1)
                    settled(eng, groups_done, i * (2 * GPH) + (GPH + SETS))
                    with eng.If(i < NH2 - 1):
                        load(i * 2 + 2, 0)
                    settled(eng, o_ready, i * 2 + 2)
                    store(i * 2, 0)
                eng.wait_ge(o_ready, H + 1)
                store(H - 1, 1)
                for p in range(2):
                    eng.wait_ge(o_stored[p], 16 * B * (NH2 + 1))

            @block.gpsimd
            def _(eng):
                def copy_v(h, p):
                    if not isinstance(h, int):
                        h = nc.s_assert_within(h, 0, H - 1, skip_runtime_bounds_check_because="the branches around it keep it in range")
                    eng.tensor_copy(vst[p][:, :, 0:HD], v_all[:, :, :].rearrange("p n (h d) -> p h n d", d=HD)[:, h])\
                       .then_inc(vst_in, 1)
                copy_v(0, 0)
                with eng.Fori(0, NH2) as i:
                    settled(eng, groups_done, i * (2 * GPH) + SETS)
                    copy_v(i * 2 + 1, 1)
                    settled(eng, groups_done, i * (2 * GPH) + (GPH + SETS))
                    with eng.If(i < NH2 - 1):
                        copy_v(i * 2 + 2, 0)

            @block.tensor
            def _(eng):
                def scores(i, g, b):
                    p, t = (g // GPH) % 2, g % GPH
                    by_vector = b < DPG
                    if b == 0 and t == 0:
                        eng.wait_ge(head_in[p], (i + (g // (2 * GPH))) * (16 * LOADS) + 16 * LOADS)
                    if by_vector:
                        k = DPG * g + b
                        u = unit(k)
                        if k >= 2:
                            eng.wait_ge(z_ready, i * (2 * DPH) + (k - 1))
                    else:
                        u = 4
                        if g:
                            eng.wait_ge(p_ready, i * (8 * GPH) + 4 * g)
                    keys = slice(b * S + t * P, b * S + (t + 1) * P)
                    for c in range(2):
                        last = eng.matmul(ps[:, u + c, :], kb[p][:, keys],
                                          qb[p][:, b * S + c * HALF:b * S + (c + 1) * HALF],
                                          start=True, stop=True)
                    if by_vector:
                        last.then_inc(sd_ready, 1)
                        return
                    for c in range(2):
                        for m in range(2):
                            c0 = t * P + 64 * m + c * HALF
                            last = eng.matmul(ps[64 * m:64 * m + 64, u + c, :], ident2[:, :],
                                              t64[p][:, c0:c0 + HALF], start=False, stop=True,
                                              skip_group_check=True)
                    last.then_inc(sp_ready, 1)

                def products(i, g, c):
                    p, t = (g // GPH) % 2, g % GPH
                    if c == 0:
                        eng.wait_ge(p_ready, i * (8 * GPH) + 4 * (g + 1))
                        if t == 0:
                            eng.wait_ge(vst_in, i * 2 + (p + 1))
                            eng.wait_ge(o_ready, i * 2 + (p + 1))
                    for b in range(B):
                        last = eng.matmul(ps[32 * b:32 * b + 32, 6 + c, :], vst[p][:, b * TB + t, :],
                                          slot(g, b)[:, c * HALF:(c + 1) * HALF],
                                          start=(t == 0), stop=(t == TB - 1))
                    if c == 1:
                        last.then_inc(groups_done, 1)

                for g in range(LAG):
                    for b in range(B):
                        scores(0, g, b)
                with eng.Fori(0, NH2) as i:
                    for g in range(2 * GPH):
                        for steps, c in (((0,), 0), ((1,), 1), ((2, 3), None)):
                            if g < 2 * GPH - LAG:
                                for b in steps:
                                    scores(i, g + LAG, b)
                            else:
                                with eng.If(i < NH2 - 1):
                                    for b in steps:
                                        scores(i, g + LAG, b)
                            if c is not None:
                                products(i, g, c)

            @block.vector
            def _(eng):
                def add_bias(i, g, b):
                    p, t, k = (g // GPH) % 2, g % GPH, DPG * g + b
                    eng.wait_ge(sd_ready, i * (2 * DPH) + (k + 1))
                    if b == 0:
                        eng.wait_ge(groups_done, i * (2 * GPH) + (g + 1))
                    eng.tensor_tensor(slot(g, b), banks(unit(k), 2), t128[p][:, t * P:t * P + S],
                                      ALU.add).then_inc(z_ready, 1)

                with eng.Fori(0, NH2) as i:
                    for g in range(2 * GPH):
                        for b in range(DPG):
                            add_bias(i, g, b)
                        if g == LAG - 1:
                            with eng.If(i > 0):
                                eng.wait_ge(groups_done, i * (2 * GPH) + SETS)
                                eng.wait_ge(o_stored[1], i * (16 * B))
                                eng.tensor_copy(o_sb[1][:, ::-1], acc).then_inc(o_ready, 1)
                        if g == GPH + LAG - 1:
                            eng.wait_ge(groups_done, i * (2 * GPH) + (GPH + SETS))
                            eng.wait_ge(o_stored[0], i * (16 * B) + 16 * B)
                            eng.tensor_copy(o_sb[0][:, ::-1], acc).then_inc(o_ready, 1)
                eng.wait_ge(groups_done, H * GPH + SETS)
                eng.wait_ge(o_stored[1], NH2 * 16 * B)
                eng.tensor_copy(o_sb[1][:, ::-1], acc).then_inc(o_ready, 1)

            @block.scalar
            def _(eng):
                with eng.Fori(0, NH2) as i:
                    for g in range(2 * GPH):
                        for b in range(B):
                            buf = slot(g, b)
                            if b < DPG:
                                eng.wait_ge(z_ready, i * (2 * DPH) + (DPG * g + b + 1))
                                eng.activation(buf, buf, ACT.Exp).then_inc(p_ready, 1)
                                continue
                            eng.wait_ge(sp_ready, i * (2 * GPH) + (g + 1))
                            eng.wait_ge(groups_done, i * (2 * GPH) + (g + 1))
                            eng.activation(buf, banks(4, 2), ACT.Exp).then_inc(p_ready, 1)

        num = [pbuf[:, b, :] for b in range(B)]
        den = [pbuf[:, B + b, :] for b in range(B)]
        PAIR = 2
        NP = NT // PAIR
        gate = o_sbs[:, :, :].rearrange("p a (n c) -> p (a n) c", c=PAIR * D)
        NG = 8
        xn2 = splitf[:, 0:NTOK].rearrange("p (n d) -> p n d", d=D)
        xn2T = splitf[:, NTOK:2 * NTOK]
        expo = v_all[:, :, :].rearrange("p n d -> p (n d)")
        x8T = qb[0][:, :].bitcast(BF16)
        yb = kb[0][:, :].bitcast(BF16)
        w8T = sb("w8T", [P, D], BF16)
        wv = sb("wv", [P, D], F32)
        wexpo = sb("wexpo", [P, D], F32)
        wv2 = sb("wv2", [P, D], F32)
        amax = sb("amax", [P, 4], F32)
        srow = sb("srow", [1, 8], F32)
        scol = sb("scol", [P, 4], F32)

        num_in = [sem(f"num_in{b}") for b in range(B)]
        attn_ready = sem("attn_ready")
        gated = sem("gated")
        sig_ready = sem("sig_ready")
        prod_ready = sem("prod_ready")
        x1_ready = sem("x1_ready")
        var2_ready = sem("var2_ready")
        std2_ready = sem("std2_ready")
        xn2_ready = sem("xn2_ready")
        xn2T_ps = sem("xn2T_ps")
        xn2T_ready = sem("xn2T_ready")
        amax_ready = sem("amax_ready")
        wT_ps = sem("wT_ps")
        amaxT_ps = sem("amaxT_ps")
        srow_ready = sem("srow_ready")
        scol_ps = sem("scol_ps")
        scol_ready = sem("scol_ready")
        xs_ready = sem("xs_ready")
        x8_ready = sem("x8_ready")
        w8_ready = sem("w8_ready")
        y_ps = sem("y_ps")
        y_ready = sem("y_ready")
        out_ready = sem("out_ready")
        out_stored = sem("out_stored")
        out_t = out.rearrange("b (n p) d -> p (b n) d", p=P)

        def tiles(b):
            return slice(b * TB, (b + 1) * TB)

        def cols(b):
            return slice(b * S, (b + 1) * S)

        with nc.Block() as block:
            @block.sync
            def _(eng):
                for b in range(B):
                    eng.dma_start(num[b], o_dram[b, :, 0:HD, :])\
                       .then_inc(num_in[b], 16)
                    dd = o_dram[b, :, HD, :]
                    eng.dma_start(den[b],
                                  bass.AP(tensor=dd.tensor, offset=dd.offset,
                                          ap=[[(HD + 1) * S, H], [0, HD], [1, S]])).then_inc(num_in[b], 16)
                for b in range(B):
                    eng.wait_ge(out_ready, b + 1)
                    eng.dma_start(out_t[:, tiles(b), :], x_sb[:, tiles(b), :]).then_inc(out_stored, 16)
                eng.wait_ge(out_stored, 16 * B)

            @block.gpsimd
            def _(eng):
                for j in range(NP):
                    eng.wait_ge(prod_ready, j + 1)
                    xs = x_sb[:, PAIR * j:PAIR * (j + 1), :].rearrange("p n d -> p (n d)")
                    eng.tensor_tensor(xs, xs, gate[:, j % NG, :], ALU.add).then_inc(x1_ready, 1)
                for b in range(B):
                    eng.wait_ge(y_ready, b + 1)
                    xs = x_sb[:, tiles(b), :].rearrange("p n d -> p (n d)")
                    eng.tensor_tensor(xs, xs, yb[:, cols(b)], ALU.add).then_inc(out_ready, 1)

            @block.tensor
            def _(eng):
                for j in range(NP):
                    if (j * PAIR) % TB == 0:
                        eng.wait_ge(attn_ready, j * PAIR // TB + 1)
                    if j >= 4:
                        eng.wait_ge(prod_ready, j - 3)
                        eng.wait_ge(sig_ready, j - 3)
                    for m in range(PAIR):
                        n = PAIR * j + m
                        dst = ps[:, j % 4, m * 2 * D:(m + 1) * 2 * D]
                        eng.matmul(dst, num[n // TB][:, (n % TB) * P:(n % TB + 1) * P], wgate[:, :],
                                   start=True, stop=False)
                        last = eng.matmul(dst, bg_ones[:, :], bg_rows[:, :], start=False, stop=True)
                    last.then_inc(gated, 1)
                eng.transpose(ps[:, 4, 0:P], wffn[:, :], ident[:, :]).then_inc(wT_ps, 1)
                for b in range(B):
                    eng.wait_ge(xn2_ready, b + 1)
                    if b == 0:
                        eng.wait_ge(prod_ready, NP)
                    if b >= 2:
                        eng.wait_ge(xn2T_ready, b - 1)
                    for n in range(TB):
                        last = eng.transpose(banks(2 * (b % 2), 2)[:, n * P:(n + 1) * P],
                                             xn2[:, b * TB + n, :], ident[:, :])
                    last.then_inc(xn2T_ps, 1)
                eng.wait_ge(amax_ready, 1)
                eng.transpose(ps[0:2, 5, 0:P], amax[:, 0:2], ident[:, :]).then_inc(amaxT_ps, 1)
                eng.wait_ge(srow_ready, 1)
                eng.transpose(ps[0:1, 6, 0:2], amax[0:2, 2:3], ident[0:2, 0:2]).then_inc(amaxT_ps, 1)
                eng.wait_ge(srow_ready, 2)
                eng.matmul(ps[:, 7, 0:4], ones_row[:, :], srow[:, 0:4], start=True, stop=True).then_inc(scol_ps, 1)
                eng.wait_ge(w8_ready, 1)
                for b in range(B):
                    eng.wait_ge(x8_ready, b + 1)
                    if b == 0:
                        eng.wait_ge(xn2T_ready, B)
                    if b >= 2:
                        eng.wait_ge(y_ready, b - 1)
                    for n in range(TB):
                        last = eng.matmul(banks(2 * (b % 2), 2)[:, n * D:(n + 1) * D],
                                          x8T[:, b * S + n * P:b * S + (n + 1) * P], w8T[:, :],
                                          start=True, stop=True)
                    last.then_inc(y_ps, 1)

            @block.scalar
            def _(eng):
                for j in range(NP):
                    eng.wait_ge(gated, j + 1)
                    if j >= NG:
                        eng.wait_ge(x1_ready, j - NG + 1)
                    eng.activation(gate[:, j % NG, :].rearrange("p (m d) -> p m d", d=D),
                                   ps[:, j % 4, :].rearrange("p (m c) -> p m c", c=2 * D)[:, :, D:2 * D],
                                   ACT.Sigmoid).then_inc(sig_ready, 1)
                eng.wait_ge(var2_ready, 1)
                eng.activation(st[:, 2, :], st[:, 1, :], ACT.Sqrt).then_inc(std2_ready, 1)
                for b in range(B):
                    eng.wait_ge(xn2T_ps, b + 1)
                    eng.activation(xn2T[:, cols(b)], banks(2 * (b % 2), 2), ACT.Copy).then_inc(xn2T_ready, 1)
                eng.wait_ge(scol_ready, 1)
                eng.activation(wv[:, :], ps[:, 4, 0:P], ACT.Copy, scale=scol[:, 2:3]).then_inc(xs_ready, 1)
                for b in range(B):
                    eng.wait_ge(xn2T_ready, b + 1)
                    eng.activation(xn2T[:, cols(b)], xn2T[:, cols(b)], ACT.Copy, scale=scol[:, 0:1])\
                       .then_inc(xs_ready, 1)

            @block.vector
            def _(eng):
                for b in range(B):
                    eng.wait_ge(num_in[b], 32)
                    chain(eng, eng.reciprocal(den[b], den[b]))
                    eng.tensor_tensor(num[b], num[b], den[b], ALU.mult).then_inc(attn_ready, 1)
                for j in range(NP + 2):
                    if j < NP:
                        eng.wait_ge(sig_ready, j + 1)
                        eng.tensor_tensor(gate[:, j % NG, :].rearrange("p (m d) -> p m d", d=D),
                                          ps[:, j % 4, :].rearrange("p (m c) -> p m c", c=2 * D)[:, :, 0:D],
                                          gate[:, j % NG, :].rearrange("p (m d) -> p m d", d=D),
                                          ALU.mult).then_inc(prod_ready, 1)
                    if j >= 2:
                        eng.wait_ge(x1_ready, j - 1)
                        for n in range(PAIR * (j - 2), PAIR * (j - 1)):
                            last = eng.bn_stats(stats[:, n, :], x_sb[:, n, :])
                chain(eng, last)
                moments(eng, slice(0, NT), var2_ready)
                eng.wait_ge(std2_ready, 1)
                chain(eng, eng.reciprocal(st[:, 3, :], st[:, 2, :]))
                for b in range(B):
                    for n in range(b * TB, (b + 1) * TB):
                        last = eng.tensor_scalar(xn2[:, n, :], x_sb[:, n, :], st[:, 0, n:n + 1],
                                                 st[:, 3, n:n + 1], ALU.subtract, ALU.mult)
                    last.then_inc(xn2_ready, 1)
                eng.wait_ge(xn2_ready, B)
                eng.tensor_reduce(amax[:, 1:2], wffn[:, :], AX.X, ALU.max, apply_absolute_value=True)
                eng.tensor_reduce(amax[:, 0:1], xn2, AX.XY, ALU.max, apply_absolute_value=True)\
                   .then_inc(amax_ready, 1)
                eng.wait_ge(amaxT_ps, 1)
                eng.tensor_reduce(amax[0:2, 2:3], ps[0:2, 5, 0:P], AX.X, ALU.max).then_inc(srow_ready, 1)
                eng.wait_ge(amaxT_ps, 2)
                chain(eng, eng.tensor_scalar(srow[:, 4:6], ps[0:1, 6, 0:2], 1e-12, None, ALU.max))
                chain(eng, eng.reciprocal(srow[:, 4:6], srow[:, 4:6]))
                chain(eng, eng.tensor_scalar(srow[:, 0:4:2], srow[:, 4:6], FP8_MAX, FP8_MAX, ALU.mult, ALU.min))
                eng.reciprocal(srow[:, 1:4:2], srow[:, 0:4:2]).then_inc(srow_ready, 1)
                eng.wait_ge(scol_ps, 1)
                eng.tensor_copy(scol[:, :], ps[:, 7, 0:4]).then_inc(scol_ready, 1)
                eng.wait_ge(scol_ready, 1)
                chain(eng, eng.tensor_tensor(scol[:, 3:4], scol[:, 3:4], scol[:, 1:2], ALU.mult))

                def quantise(v, c, dst, done):
                    chain(eng, eng.tensor_scalar(c.bitcast(I32), v.bitcast(I32), 0x7F800000, None,
                                                 ALU.bitwise_and))
                    chain(eng, eng.tensor_scalar(c, c, 2.0 ** -6, 1.5 * 2.0 ** 20, ALU.max, ALU.mult))
                    chain(eng, eng.tensor_tensor(v, v, c, ALU.add))
                    chain(eng, eng.tensor_tensor(dst, v, c, ALU.subtract))
                    eng.tensor_scalar(dst, dst, FP8_MAX, -FP8_MAX, ALU.min, ALU.max).then_inc(done, 1)

                def finish(b):
                    eng.wait_ge(y_ps, b + 1)
                    eng.scalar_tensor_tensor(out=yb[:, cols(b)].rearrange("p (n d) -> p n d", d=D),
                                             in0=banks(2 * (b % 2), 2).rearrange("p (n d) -> p n d", d=D),
                                             scalar=scol[:, 3:4],
                                             in1=bass.AP(tensor=ffn_bias[:, :].tensor, offset=ffn_bias[:, :].offset,
                                                         ap=[list(ffn_bias[:, :].ap[0]), [0, TB], [1, D]]),
                                             op0=ALU.mult, op1=ALU.add).then_inc(y_ready, 1)

                eng.wait_ge(xs_ready, 1)
                quantise(wv[:, :], wexpo[:, :], w8T[:, :], w8_ready)
                for b in range(B):
                    eng.wait_ge(xs_ready, b + 2)
                    quantise(xn2T[:, cols(b)], expo[:, cols(b)], x8T[:, cols(b)], x8_ready)
                    if b:
                        finish(b - 1)
                finish(B - 1)


_INS = {"L0_attn_x": "x", "L0_attn_w_in": "w_in", "L0_attn_w_gate": "w_gate", "L0_attn_b_gate": "b_gate",
        "L0_attn_amplitudes": "amplitudes", "L0_attn_sharpness": "sharpness", "L0_attn_offsets": "offsets",
        "L0_ffn_weight": "w_ffn", "L0_ffn_bias": "ffn_bias"}


def kernel(**inputs):
    import numpy as np
    import concourse.bacc as bacc
    from concourse.bass_utils import run_bass_kernel_spmd

    pair = np.arange(PAIRS).reshape(PG, PP).T // KB
    consts = {
        "c_ident": np.eye(P, dtype=np.float32),
        "c_ident2": np.concatenate([np.eye(64), np.eye(64)]).astype(np.float16),
        "c_sel": (pair[:, :, None] == np.arange(32)).astype(np.float32),
        "c_hsel": (np.arange(P)[:, None] // HD == np.arange(32)).astype(np.float32),
        "c_rel": (np.arange(GN) - (S - 1)).astype(np.float32),
    }
    nc = bacc.Bacc("TRN2", target_bir_lowering=False, num_devices=1)
    arrays = {f"in_{name}": np.ascontiguousarray(inputs[name]) for name in _INS}
    arrays.update(consts)
    io = {}
    for name, a in arrays.items():
        short = _INS[name[3:]] if name[3:] in _INS else name
        io[short] = nc.dram_tensor(name, a.shape, mybir.dt.from_np(a.dtype), kind="ExternalInput").ap()
    out = nc.dram_tensor("out_0", (B, S, D), F32, kind="ExternalOutput").ap()
    attention_block(nc, io, out)
    r = run_bass_kernel_spmd(nc, [arrays], core_ids=[0])
    return r.results[0]["out_0"]
```

```python
from contextlib import ExitStack

import numpy as np

import concourse.bass as bass
from concourse import mybir

F32 = mybir.dt.float32
F16 = mybir.dt.float16
BF16 = mybir.dt.bfloat16
I32 = mybir.dt.int32
ALU = mybir.AluOpType
ACT = mybir.ActivationFunctionType
AX = mybir.AxisListType

B, S, D = 4, 1024, 128
H, KB = 16, 21
HD = D // H
P = 128
NTOK = B * S
NT = NTOK // P
TB = S // P
HALF = 512
PAIRS = H * KB
PG = 3
PP = PAIRS // PG
GN = 2 * S
T128W = 2 * S - P
T64W = 2 * S - 64
NH2 = H // 2
VW = 32
EPS = 1e-5
QSCALE = float(HD) ** -0.5
SAFE = 60.0
FP8_MAX = 448.0
DPG = 3
WARM_START = 26
WARM_GATE = 48
SETS = 4
LAG = 2
DPH = DPG * TB


def attention_block(nc, io, out):
    with ExitStack() as ctx:
        def sb(name, shape, dt):
            return ctx.enter_context(nc.sbuf_tensor(name, shape, dt))

        def sem(name):
            return ctx.enter_context(nc.semaphore(name))

        def dram(name, shape, dt):
            return nc.dram_tensor(name, shape, dt, kind="Internal").ap()

        q_dram = dram("q_scratch", [2, P, NTOK], F16)
        k_dram = dram("k_scratch", [2, P, NTOK], F16)
        g_dram = dram("g_scratch", [32, GN], F32)
        gh_dram = dram("gh_scratch", [32, GN], F16)
        gl_dram = dram("gl_scratch", [32, GN], F16)
        m_dram = dram("m_scratch", [H, NTOK], F16)
        o_dram = dram("o_scratch", [B, H, HD, S], F32)
        r_dram = dram("r_scratch", [2, B, S], F32)
        bg_dram = dram("bg_scratch", [3, 2 * D], BF16)

        x_sb = sb("x_sb", [P, NT, D], F32)
        ident = sb("ident", [P, P], F32)
        win = sb("win", [P, 3 * D], F32)
        wgate = sb("wgate", [P, 2 * D], F32)
        wffn = sb("wffn", [P, D], F32)
        ffn_bias = sb("ffn_bias", [P, D], F32)
        bgate = sb("bgate", [1, 2 * D], F32)
        bg_parts = sb("bg_parts", [1, 3, 2 * D], BF16)
        bg_rows = sb("bg_rows", [3, 2 * D], BF16)
        ones_row = sb("ones_row", [1, P], F32)
        bg_ones = sb("bg_ones", [3, P], BF16)
        ident2 = sb("ident2", [P, 64], F16)
        v_all = sb("v_all", [P, NT, D], F32)
        stats = sb("stats", [P, NT, 6], F32)
        mv = sb("mv", [P, NT, 2], F32)
        minus_half = sb("minus_half", [P, NT], F32)
        st = sb("st", [P, 2, NT], F32)
        flag = sb("flag", [1, 1], I32)
        small = sb("small", [P, 32], F32)
        qb = [sb(f"qb{p}", [P, NTOK], F16) for p in range(2)]
        kb = [sb(f"kb{p}", [P, NTOK], F16) for p in range(2)]
        t64s = sb("t64s", [P, 2, 2 * S], F16)
        t64 = [t64s[:, p, :] for p in range(2)]
        t128 = [sb(f"t128_{p}", [P, 2 * S], F32) for p in range(2)]
        vst = [sb(f"vst{p}", [P, NT, VW], F32) for p in range(2)]
        pbuf = sb("pbuf", [P, 8, S], F32)
        dc = [sb(f"dc{p}", [P, B * S // P], F32) for p in range(2)]
        rd = sb("rd", [P, S], F32)
        o_sbs = sb("o_sbs", [P, 2, S], F32)
        o_sb = [o_sbs[:, p, :] for p in range(2)]
        big = pbuf[:, :, :].rearrange("p a c -> p (a c)")
        xn = big[:, 0:NTOK].rearrange("p (n d) -> p n d", d=D)
        xT = big[:, NTOK:2 * NTOK]
        split = sb("split", [P, 4, NTOK], F16)
        splitf = split[:, :, :].rearrange("p a c -> p (a c)").bitcast(F32)
        gauss = [t128[0][0:PP, :], t128[1][0:PP, :], o_sbs[0:PP, :, :].rearrange("p a c -> p (a c)")]
        ps = ctx.enter_context(nc.psum_tensor("ps", [P, 8, HALF], F32))

        def banks(a, n):
            return ps[:, a:a + n, :].rearrange("p a c -> p (a c)")

        amp = sb("amp", [PP, PG], F32)
        shp = sb("shp", [PP, PG], F32)
        off = sb("off", [PP, PG], F32)
        nshp = sb("nshp", [PP, PG], F32)
        noff = sb("noff", [PP, PG], F32)
        sel = sb("sel", [PP, PG, 32], F32)
        rel = t64s[0:PP, :, :].rearrange("p a c -> p (a c)").bitcast(F32)
        zeros = sb("zeros", [P, HALF], F16)
        hsel = sb("hsel", [P, 32], F32)
        hselb = sb("hselb", [P, 32], BF16)
        sq = [xn[:, b * TB:(b + 1) * TB, :].rearrange("p n d -> p (n d)").bitcast(BF16)
              .rearrange("p (i c) -> p i c", i=2) for b in range(B)]
        gv = sb("gv", [P, HALF], F32)
        gvh = sb("gvh", [P, HALF], F16)
        gvl = sb("gvl", [P, HALF], F16)
        bnd = sb("bnd", [P, 4], F32)
        bndr = sb("bndr", [4, 1], F32)
        bndt = sb("bndt", [1, 4], F32)
        dve_done = sem("dve_done")
        dve_count = [0]

        def chain(eng, ins):
            dve_count[0] += 1
            ins.then_inc(dve_done, 1)
            eng.wait_ge(dve_done, dve_count[0])

        x_in = [sem(f"x_in{b}") for b in range(B)]
        ident_in = sem("ident_in")
        win_in = sem("win_in")
        consts_in = sem("consts_in")
        rel_in = sem("rel_in")
        par_in = sem("par_in")
        sel_in = sem("sel_in")
        sel_ready = sem("sel_ready")
        par_ready = sem("par_ready")
        stats_ready = sem("stats_ready")
        var_ready = sem("var_ready")
        rstd_ready = sem("rstd_ready")
        xn_ready = sem("xn_ready")
        xnT_ready = sem("xnT_ready")
        xT_ready = sem("xT_ready")
        q_ready = sem("q_ready")
        k_ready = sem("k_ready")
        v_ready = sem("v_ready")
        qh_ready = sem("qh_ready")
        kh_ready = sem("kh_ready")
        v_copied = sem("v_copied")
        ql_ready = sem("ql_ready")
        kl_ready = sem("kl_ready")
        sq_ready = sem("sq_ready")
        sqk_ready = sem("sqk_ready")
        norm_ready = sem("norm_ready")
        square_ready = sem("square_ready")
        exp_ready = sem("exp_ready")
        gsum_ready = sem("gsum_ready")
        gh_ready = sem("gh_ready")
        gl_ready = sem("gl_ready")
        bnd_ready = sem("bnd_ready")
        bndT_ready = sem("bndT_ready")
        bndr_ready = sem("bndr_ready")
        bndt_ready = sem("bndt_ready")
        m_out = sem("m_out")
        bg_out = sem("bg_out")
        qk_out = sem("qk_out")
        g_out = sem("g_out")
        filled = sem("filled")
        hsel_ready = sem("hsel_ready")
        bg_ready = sem("bg_ready")
        head_in = [sem(f"head_in{p}") for p in range(2)]
        first_in = sem("first_in")
        vst_in = sem("vst_in")
        groups_done = sem("groups_done")
        o_ready = [sem(f"o_ready{c}") for c in range(2)]
        o_stored = [sem(f"o_stored{p}") for p in range(2)]
        g_row = sem("g_row")
        g_stored = sem("g_stored")

        def tiles(b):
            return slice(b * TB, (b + 1) * TB)

        def cols(b):
            return slice(b * S, (b + 1) * S)

        def back(b):
            return slice(S - 1 + b * S, b * S - 1 if b else None, -1)

        def slice_of(t, h, rows, width):
            v = t[h, :]
            return bass.AP(tensor=v.tensor, offset=v.offset, ap=[[1, rows], [1, width]])

        def load_bias(eng, h, p, done):
            eng.dma_start(t128[p][:, 0:T128W], slice_of(g_dram, h, P, T128W)).then_inc(done, 16)

        def load_bias_parts(eng, h, p, done):
            eng.dma_start(t64[p][0:64, 0:T64W], slice_of(gh_dram, h, 64, T64W)).then_inc(done, 16)
            eng.dma_start(t64[p][64:P, 0:T64W], slice_of(gl_dram, h, 64, T64W)).then_inc(done, 16)

        def load_qk(eng, h, p, done):
            for rep in range(2):
                eng.dma_start(qb[p][16 * rep:16 * rep + 16, :],
                              q_dram.rearrange("a (h d) n -> h a d n", d=HD)[h]).then_inc(done, 16)
            for hl in range(2):
                for rep in range(2):
                    r = 16 * hl + 8 * rep
                    eng.dma_start(kb[p][r:r + 8, :],
                                  k_dram.rearrange("a (h d) n -> h a d n", d=HD)[h, hl]).then_inc(done, 16)

        def store_qk(eng, b, done):
            for ready, part, dst, hl in ((qh_ready, 0, q_dram, 0), (kh_ready, 2, k_dram, 0),
                                         (ql_ready, 1, q_dram, 1), (kl_ready, 3, k_dram, 1)):
                eng.wait_ge(ready, b + 1)
                eng.dma_start(dst[hl, :, cols(b)], split[:, part, cols(b)]).then_inc(done, 16)

        def load_maxima(eng, h, p, done):
            eng.dma_start(qb[p][32:33, :], m_dram[h, :].rearrange("(a n) -> a n", a=1)).then_inc(done, 16)
        LOADS = 10
        QK_LOADS = 6
        LOADS_G = 7

        def copy_v(eng, h, p):
            eng.tensor_copy(vst[p][:, :, 0:HD], v_all[:, :, :].rearrange("p n (h d) -> p h n d", d=HD)[:, h])\
               .then_inc(vst_in, 1)

        x_t = io["x"].rearrange("b (n p) d -> p (b n) d", p=P)
        NEG1_PAIR = float(np.array([-1.0, -1.0], np.float16).view(np.float32)[0])
        fills = [[(zeros[:, :].bitcast(F32), 0.0), (minus_half[:, :], -0.5), (ones_row[:, :], 1.0),
                  (bg_ones[:, :], 1.0)], []]
        for p in range(2):
            for t in (qb[p], kb[p]):
                fills[p].append((t[32:64, :].bitcast(F32), 0.0))
                fills[p].append((t[64:P, :].bitcast(F32), 0.0))
            fills[p].append((kb[p][32:33, :].bitcast(F32), NEG1_PAIR))
            fills[p].append((vst[p][:, :, :], 0.0))
            fills[p].append((vst[p][:, :, HD:HD + 1], 1.0))
        fills[1].append((rd[:, :], 1.0))
        FILLS0 = len(fills[0])
        FILLS = FILLS0 + len(fills[1])

        with nc.Block() as block:
            @block.sync
            def _(eng):
                def load_x(b):
                    eng.dma_start(x_sb[:, tiles(b), :], x_t[:, tiles(b), :]).then_inc(x_in[b], 16)

                load_x(0)
                with nc.allow_non_contiguous_dma(reason="336 parameters"):
                    for dst, name in ((off, "offsets"), (shp, "sharpness"), (amp, "amplitudes")):
                        eng.dma_start(dst[:, :], io[name].rearrange("h k -> (h k)")
                                      .rearrange("(g p) -> p g", p=PP)).then_inc(par_in, 16)
                load_x(1)
                eng.dma_start(rel, bass.AP(tensor=io["c_rel"].tensor, offset=0,
                                           ap=[[0, PP], [1, GN]])).then_inc(rel_in, 16)
                eng.dma_start(sel[:, :, :], io["c_sel"]).then_inc(sel_in, 16)
                eng.dma_start(hsel[:, :], io["c_hsel"]).then_inc(sel_in, 16)
                load_x(2)
                load_x(3)
                eng.dma_start(ident2[:, :], io["c_ident2"]).then_inc(consts_in, 16)
                eng.dma_start(bgate[:, :], io["b_gate"].rearrange("(a n) -> a n", a=1)).then_inc(consts_in, 16)
                eng.dma_start(wffn[:, :], io["w_ffn"]).then_inc(consts_in, 16)
                eng.dma_start(wgate[:, :], io["w_gate"]).then_inc(consts_in, 16)
                eng.dma_start(ffn_bias[:, :], bass.AP(tensor=io["ffn_bias"].tensor, offset=0,
                                                      ap=[[0, P], [1, D]])).then_inc(consts_in, 16)
                eng.wait_ge(filled, 1)
                eng.dma_start(m_dram.rearrange("h (a c) -> (h a) c", c=HALF), zeros[:, :]).then_inc(m_out, 16)

                store_qk(eng, 0, qk_out)
                eng.wait_ge(gh_ready, 1)
                eng.wait_ge(gl_ready, 1)
                for src, dst in ((gv, g_dram), (gvh, gh_dram), (gvl, gl_dram)):
                    eng.dma_start(dst.rearrange("h (c n) -> c h n", n=HALF), src[:, :]).then_inc(g_out, 16)
                store_qk(eng, 1, qk_out)
                eng.wait_ge(filled, FILLS0)
                eng.wait_ge(m_out, 16)
                load_maxima(eng, 0, 0, head_in[0])
                eng.wait_ge(g_out, 16 * 3)
                load_bias(eng, 0, 0, head_in[0])
                load_bias_parts(eng, 0, 0, head_in[0])
                for ready, part, dst, rows in ((qh_ready, 0, qb[0], (0, 16)), (ql_ready, 1, qb[0], (8, 24)),
                                               (kh_ready, 2, kb[0], (0, 8)), (kl_ready, 3, kb[0], (16, 24))):
                    eng.wait_ge(ready, B)
                    for r in rows:
                        eng.dma_start(dst[r:r + HD, :], split[0:HD, part, :]).then_inc(first_in, 16)

            @block.gpsimd
            def _(eng):
                count = [0]

                def fill(n):
                    for dst, value in fills[0][count[0]:count[0] + n]:
                        if count[0]:
                            eng.wait_ge(filled, count[0])
                        eng.memset(dst, value).then_inc(filled, 1)
                        count[0] += 1

                def inverse_std(b):
                    eng.wait_ge(filled, count[0])
                    eng.wait_ge(var_ready, b + 1)
                    eng.tensor_scalar(st[:, 1, tiles(b)], mv[:, tiles(b), 1], EPS, None, ALU.add)\
                       .then_inc(rstd_ready, 1)
                    eng.wait_ge(rstd_ready, 2 * b + 1)
                    eng.tensor_tensor(st[:, 0, tiles(b)], st[:, 1, tiles(b)], minus_half[:, tiles(b)], ALU.pow)\
                       .then_inc(rstd_ready, 1)

                def square(b, i, ready):
                    part = split[:, 2 * i, cols(b)]
                    eng.wait_ge(filled, count[0])
                    eng.wait_ge(ready, b + 1)
                    eng.tensor_tensor(sq[b][:, i, :], part, part, ALU.mult).then_inc(sq_ready, 1)

                fill(6)
                inverse_std(0)
                eng.wait_ge(rstd_ready, 2)
                fill(1)
                inverse_std(1)
                eng.wait_ge(rstd_ready, 4)
                fill(2)
                inverse_std(2)
                square(0, 0, qh_ready)
                eng.wait_ge(rstd_ready, 6)
                eng.wait_ge(sq_ready, 1)
                fill(2)
                square(0, 1, kh_ready)
                inverse_std(3)
                square(1, 0, qh_ready)
                eng.sem_inc(groups_done, SETS)
                eng.sem_inc(o_stored[0], 16 * B)
                eng.sem_inc(o_stored[1], 16 * B)
                eng.sem_inc(o_ready[0], 1)
                eng.sem_inc(o_ready[1], 1)
                eng.sem_inc(g_row, 1)
                eng.sem_inc(g_stored, 16)
                square(2, 0, qh_ready)
                square(3, 0, qh_ready)
                eng.wait_ge(v_copied, B)
                copy_v(eng, 0, 0)

            @block.scalar
            def _(eng):
                eng.dma_start(ident[:, :], io["c_ident"]).then_inc(ident_in, 16)
                eng.dma_start(win[:, :], io["w_in"]).then_inc(win_in, 16)

                def square(g):
                    if g == 0:
                        eng.wait_ge(rel_in, 16)
                        eng.wait_ge(par_ready, 1)
                    eng.activation(gauss[g], rel, ACT.Square, bias=noff[:, g:g + 1]).then_inc(square_ready, 1)

                def gaussian(g):
                    eng.wait_ge(square_ready, g + 1)
                    eng.activation(gauss[g], gauss[g], ACT.Exp, scale=nshp[:, g:g + 1]).then_inc(exp_ready, 1)

                def turn(b):
                    eng.wait_ge(xnT_ready, b + 1)
                    eng.activation(xT[:, cols(b)], banks(0, 2), ACT.Copy).then_inc(xT_ready, 1)

                def q_high(b):
                    eng.wait_ge(q_ready, b + 1)
                    eng.activation(split[:, 0, back(b)], banks(2, 2), ACT.Copy, scale=QSCALE).then_inc(qh_ready, 1)

                def k_high(b):
                    eng.wait_ge(k_ready, b + 1)
                    eng.activation(split[:, 2, cols(b)], banks(4, 2), ACT.Copy).then_inc(kh_ready, 1)

                def v_copy(b):
                    eng.wait_ge(v_ready, b + 1)
                    eng.activation(v_all[:, tiles(b), :].rearrange("p n d -> p (n d)"), banks(6, 2), ACT.Copy)\
                       .then_inc(v_copied, 1)

                def k_square(b):
                    eng.wait_ge(kh_ready, b + 1)
                    eng.activation(sq[b][:, 1, :], split[:, 2, cols(b)], ACT.Square).then_inc(sqk_ready, 1)

                for step, n in ((square, 0), (turn, 0), (square, 1), (q_high, 0), (square, 2), (gaussian, 0),
                                (turn, 1), (k_high, 0), (v_copy, 0), (gaussian, 1), (q_high, 1), (turn, 2),
                                (gaussian, 2), (k_high, 1), (q_high, 2), (turn, 3), (v_copy, 1), (k_high, 2),
                                (k_square, 1), (q_high, 3), (v_copy, 2), (k_square, 2), (k_high, 3),
                                (k_square, 3)):
                    step(n)
                v_copy(B - 1)

            @block.vector
            def _(eng):
                def stats_of(b):
                    eng.wait_ge(x_in[b], 16)
                    for n in range(b * TB, (b + 1) * TB):
                        last = eng.bn_stats(stats[:, n, :], x_sb[:, n, :])
                    last.then_inc(stats_ready, 1)

                def moments(b):
                    eng.wait_ge(stats_ready, b + 1)
                    for n in range(b * TB, (b + 1) * TB):
                        last = eng.bn_aggr(mv[:, n, :], stats[:, n, :])
                    last.then_inc(var_ready, 1)

                def normalise(b):
                    eng.wait_ge(rstd_ready, 2 * b + 2)
                    for n in range(b * TB, (b + 1) * TB):
                        last = eng.tensor_scalar(xn[:, n, :], x_sb[:, n, :], mv[:, n, 0:1],
                                                 st[:, 0, n:n + 1], ALU.subtract, ALU.mult)
                    last.then_inc(xn_ready, 1)

                def q_low(b):
                    eng.wait_ge(qh_ready, b + 1)
                    eng.scalar_tensor_tensor(out=split[:, 1, back(b)], in0=banks(2, 2), scalar=QSCALE,
                                             in1=split[:, 0, back(b)], op0=ALU.mult, op1=ALU.subtract)\
                       .then_inc(ql_ready, 1)

                def k_low(b):
                    eng.wait_ge(kh_ready, b + 1)
                    eng.tensor_tensor(split[:, 3, cols(b)], banks(4, 2), split[:, 2, cols(b)], ALU.subtract)\
                       .then_inc(kl_ready, 1)

                stats_of(0)
                moments(0)
                eng.wait_ge(par_in, 48)
                eng.tensor_scalar(noff[:, :], off[:, :], -1.0, None, ALU.mult)
                chain(eng, eng.tensor_scalar(nshp[:, :], shp[:, :], -1.0, None, ALU.mult))
                eng.tensor_tensor(nshp[:, :], nshp[:, :], shp[:, :], ALU.min).then_inc(par_ready, 1)
                stats_of(1)
                normalise(0)
                moments(1)
                stats_of(2)
                normalise(1)
                moments(2)
                eng.wait_ge(sel_in, 32)
                eng.tensor_copy(hselb[:, :], hsel[:, :]).then_inc(hsel_ready, 1)
                for g in range(PG):
                    last = eng.tensor_scalar(sel[:, g, :], sel[:, g, :], amp[:, g:g + 1], None, ALU.mult)
                last.then_inc(sel_ready, 1)
                q_low(0)
                stats_of(3)
                normalise(2)
                k_low(0)
                moments(3)
                q_low(1)
                normalise(3)
                eng.wait_ge(gsum_ready, 1)
                chain(eng, eng.tensor_copy(gvh[:, :], ps[:, 6, :]))
                eng.tensor_copy(gv[:, :], ps[:, 6, :]).then_inc(gh_ready, 1)
                eng.tensor_tensor(gvl[:, :], ps[:, 6, :], gvh[:, :], ALU.subtract).then_inc(gl_ready, 1)
                eng.tensor_reduce(bnd[:, 2:3], ps[:, 6, :], AX.X, ALU.max, apply_absolute_value=True)\
                   .then_inc(gl_ready, 1)
                k_low(1)
                q_low(2)
                k_low(2)
                eng.wait_ge(consts_in, 80)
                chain(eng, eng.tensor_copy(bg_parts[:, 0, :], bgate[:, :]))
                chain(eng, eng.tensor_tensor(bgate[:, :], bgate[:, :], bg_parts[:, 0, :], ALU.subtract))
                chain(eng, eng.tensor_copy(bg_parts[:, 1, :], bgate[:, :]))
                chain(eng, eng.tensor_tensor(bgate[:, :], bgate[:, :], bg_parts[:, 1, :], ALU.subtract))
                eng.tensor_copy(bg_parts[:, 2, :], bgate[:, :]).then_inc(bg_ready, 1)
                q_low(3)
                k_low(3)
                eng.wait_ge(norm_ready, 1)
                eng.tensor_reduce(bnd[:, 0:1], banks(0, 2), AX.X, ALU.max)
                eng.wait_ge(norm_ready, 2)
                eng.tensor_reduce(bnd[:, 1:2], banks(2, 2), AX.X, ALU.max).then_inc(bnd_ready, 1)
                eng.wait_ge(bndT_ready, 1)
                eng.tensor_reduce(bndr[0:3, :], ps[0:3, 4, 0:P], AX.X, ALU.max).then_inc(bndr_ready, 1)
                eng.wait_ge(bndt_ready, 1)
                chain(eng, eng.tensor_copy(bndt[:, 0:3], ps[0:1, 5, 0:3]))
                eng.scalar_tensor_tensor(out=small[0:1, 0:1], in0=bndt[:, 0:1], scalar=1.05,
                                         in1=bndt[:, 1:2], op0=ALU.mult, op1=ALU.mult)
                chain(eng, eng.tensor_scalar(small[0:1, 1:2], bndt[:, 2:3], -1.0, SAFE, ALU.mult, ALU.add))
                chain(eng, eng.tensor_scalar(small[0:1, 1:2], small[0:1, 1:2], 0.0, None, ALU.max))
                chain(eng, eng.tensor_tensor(small[0:1, 2:3], small[0:1, 1:2], small[0:1, 1:2], ALU.mult))
                chain(eng, eng.tensor_tensor(small[0:1, 3:4], small[0:1, 0:1], small[0:1, 2:3], ALU.is_le))
                chain(eng, eng.tensor_scalar(flag[:, :], small[0:1, 3:4], -1.0, 1.0, ALU.mult, ALU.add))

            @block.tensor
            def _(eng):
                def turn(b):
                    if b == 0:
                        eng.wait_ge(ident_in, 16)
                    eng.wait_ge(xn_ready, b + 1)
                    if b >= 1:
                        eng.wait_ge(xT_ready, b)
                    for n in range(TB):
                        last = eng.transpose(banks(0, 2)[:, n * P:(n + 1) * P], xn[:, b * TB + n, :], ident[:, :])
                    last.then_inc(xnT_ready, 1)

                def q_of(b):
                    eng.wait_ge(xT_ready, b + 1)
                    if b == 0:
                        eng.wait_ge(win_in, 16)
                    if b >= 1:
                        eng.wait_ge(ql_ready, b)
                    for c in range(2):
                        last = eng.matmul(ps[:, 2 + c, :], win[:, 2 * D:3 * D],
                                          xT[:, b * S + c * HALF:b * S + (c + 1) * HALF], start=True, stop=True)
                    last.then_inc(q_ready, 1)

                def k_of(b):
                    if b >= 1:
                        eng.wait_ge(kl_ready, b)
                    for c in range(2):
                        last = eng.matmul(ps[:, 4 + c, :], win[:, 0:D],
                                          xT[:, b * S + c * HALF:b * S + (c + 1) * HALF], start=True, stop=True)
                    last.then_inc(k_ready, 1)

                def v_of(b):
                    if b >= 1:
                        eng.wait_ge(v_copied, b)
                    for n in range(TB):
                        last = eng.matmul(banks(6, 2)[:, n * P:(n + 1) * P],
                                          xT[:, b * S + n * P:b * S + (n + 1) * P], win[:, D:2 * D],
                                          start=True, stop=True)
                    last.then_inc(v_ready, 1)

                def bias_vectors():
                    eng.wait_ge(sel_ready, 1)
                    eng.wait_ge(v_copied, 1)
                    for g in range(PG):
                        eng.wait_ge(exp_ready, g + 1)
                        for c in range(4):
                            last = eng.matmul(ps[32 * c:32 * c + 32, 6, :], sel[:, g, :],
                                              gauss[g][:, c * HALF:(c + 1) * HALF],
                                              start=(g == 0), stop=(g == PG - 1))
                    last.then_inc(gsum_ready, 1)

                def norms(i):
                    for c in range(2):
                        for b in range(B):
                            last = eng.matmul(ps[32 * b:32 * b + 32, 2 * i + c, :], hselb[:, :],
                                              sq[b][:, i, c * HALF:(c + 1) * HALF],
                                              start=True, stop=True)
                    last.then_inc(norm_ready, 1)

                eng.wait_ge(filled, 1)
                for _ in range(WARM_START):
                    eng.matmul(ps[:, 7, :], zeros[:, 0:P], zeros[:, :], start=True, stop=True)
                turn(0)
                q_of(0)
                turn(1)
                k_of(0)
                v_of(0)
                q_of(1)
                turn(2)
                k_of(1)
                bias_vectors()
                q_of(2)
                turn(3)
                eng.wait_ge(gl_ready, 2)
                v_of(1)
                k_of(2)
                q_of(3)
                v_of(2)
                k_of(3)
                v_of(3)
                eng.wait_ge(hsel_ready, 1)
                eng.wait_ge(xT_ready, B)
                eng.wait_ge(sq_ready, B + 1)
                norms(0)
                eng.wait_ge(ql_ready, B)
                eng.wait_ge(sqk_ready, 3)
                norms(1)
                eng.wait_ge(bnd_ready, 1)
                eng.wait_ge(kl_ready, B)
                eng.transpose(ps[0:3, 4, 0:P], bnd[:, 0:3], ident[:, :]).then_inc(bndT_ready, 1)
                eng.wait_ge(bndr_ready, 1)
                eng.transpose(ps[0:1, 5, 0:3], bndr[0:3, :], ident[0:3, 0:3]).then_inc(bndt_ready, 1)

        m_sb = sb("m_sb", [P, NT], F32)
        m_row = sb("m_row", [NT, P], F16)
        g_loaded = sem("g_loaded")
        g_steps = sem("g_steps")
        g_scores = sem("g_scores")
        g_again = sem("g_again")
        g_summed = sem("g_summed")
        g_max = sem("g_max")
        g_turned = sem("g_turned")
        zsum = [pbuf[:, i, :] for i in range(2)]

        with nc.Block() as block:
            @block.sync
            def _(eng):
                f = eng.value_load(flag[0:1, 0:1], min_val=0, max_val=1)
                with eng.If(f == 1):
                    eng.wait_ge(first_in, 16 * 8)
                    eng.wait_ge(head_in[0], 16 * (LOADS - QK_LOADS))
                    for b in range(B - 2, B):
                        store_qk(eng, b, g_again)
                    eng.wait_ge(qk_out, 16 * 4 * (B - 2))
                    eng.wait_ge(g_again, 16 * 4 * 2)
                    with eng.Fori(0, H) as h:
                        eng.wait_ge(g_row, h + 1)
                        eng.sem_inc(g_steps, 1)
                        load_qk(eng, h, 0, g_loaded)
                        load_bias(eng, h, 0, g_loaded)
                        eng.wait_ge(g_row, h + 2)
                        eng.sem_inc(g_steps, 1)
                        eng.dma_start(m_dram[h, :].rearrange("(n p) -> n p", p=P), m_row[:, :])\
                           .then_inc(g_stored, 16)
                        eng.wait_ge(g_stored, h * 16 + 32)
                        eng.sem_inc(g_steps, 1)
                    load_qk(eng, 0, 0, g_again)
                    load_bias(eng, 0, 0, g_again)
                    load_maxima(eng, 0, 0, g_again)
                    eng.wait_ge(g_again, 16 * (4 * 2 + LOADS_G + 1))
                    eng.sem_inc(g_steps, 1)

            @block.tensor
            def _(eng):
                f = eng.value_load(flag[0:1, 0:1], min_val=0, max_val=1)
                with eng.If(f == 1):
                    with eng.Fori(0, H) as h:
                        eng.wait_ge(g_loaded, h * (16 * LOADS_G) + 16 * LOADS_G)
                        for n in range(NT):
                            b = n // TB
                            if n >= 2:
                                eng.wait_ge(g_summed, h * NT + (n - 1))
                            for c in range(2):
                                last = eng.matmul(ps[:, 2 * (n % 2) + c, :], qb[0][0:32, n * P:(n + 1) * P],
                                                  kb[0][0:32, b * S + c * HALF:b * S + (c + 1) * HALF],
                                                  start=True, stop=True)
                            last.then_inc(g_scores, 1)
                        eng.wait_ge(g_max, h * NT + NT)
                        eng.transpose(ps[0:NT, 4, 0:P], m_sb[:, :], ident[:, :]).then_inc(g_turned, 1)

            @block.vector
            def _(eng):
                f = eng.value_load(flag[0:1, 0:1], min_val=0, max_val=1)
                with eng.If(f == 1):
                    with eng.Fori(0, H) as h:
                        for n in range(NT):
                            c0 = (n % TB) * P
                            eng.wait_ge(g_scores, h * NT + (n + 1))
                            eng.tensor_tensor(zsum[n % 2], banks(2 * (n % 2), 2), t128[0][:, c0:c0 + S],
                                              ALU.add).then_inc(g_summed, 1)
                            eng.wait_ge(g_summed, h * NT + (n + 1))
                            eng.tensor_reduce(m_sb[:, n:n + 1], zsum[n % 2], AX.X, ALU.max).then_inc(g_max, 1)
                        eng.wait_ge(g_turned, h + 1)
                        eng.wait_ge(g_stored, h * 16 + 16)
                        eng.tensor_copy(m_row[:, :], ps[0:NT, 4, 0:P]).then_inc(g_row, 1)

        queue_steps = sem("queue_steps")
        sd_ready = sem("sd_ready")
        den_in = [sem(f"den_in{p}") for p in range(2)]
        inv_ready = [sem(f"inv_ready{p}") for p in range(2)]
        inv_out = [sem(f"inv_out{p}") for p in range(2)]
        rd_in = sem("rd_in")
        o_norm = sem("o_norm")
        half_done = sem("half_done")
        sp_ready = sem("sp_ready")
        z_ready = sem("z_ready")
        p_ready = sem("p_ready")

        GPH = TB
        def copy_half(eng, p, c):
            src, dst = ps[:, 6 + c, :], o_sb[p][:, S - 1 - c * HALF:(S - 1 - (c + 1) * HALF if c == 0 else None):-1]
            if c == 0:
                return eng.tensor_copy(dst, src)
            return eng.activation(dst, src, ACT.Copy)

        def settled(eng, s, value):
            eng.wait_ge(s, value)
            eng.sem_inc(queue_steps, 1)

        def in_range(h):
            return nc.s_assert_within(
                h, 0, H - 1, skip_runtime_bounds_check_because="the branches around it keep it in range")

        def slot(g, b):
            n = 4 * (g % SETS) + b
            return pbuf[:, n, :] if n < 8 else splitf[:, (n - 8) * S:(n - 7) * S]

        def unit(k):
            return 2 * (k % 2)

        def send_denominators(eng, p):
            eng.dma_start(dc[p][:, :], o_sb[p][HD:P:32, :]).then_inc(den_in[p], 16)

        def spread_inverses(eng, p):
            for b in range(B):
                r = r_dram[p, b]
                eng.dma_start(rd[32 * b:32 * b + HD, :],
                              bass.AP(tensor=r.tensor, offset=r.offset, ap=[[0, HD], [1, S]])).then_inc(rd_in, 16)

        with nc.Block() as block:
            @block.sync
            def _(eng):
                def load(h, p):
                    h = in_range(h)
                    load_qk(eng, h, p, head_in[p])
                    load_bias(eng, h, p, head_in[p])
                    load_bias_parts(eng, h, p, head_in[p])
                    load_maxima(eng, h, p, head_in[p])

                def normalise_and_store(h, p, before):
                    h = in_range(h)
                    send_denominators(eng, p)
                    settled(eng, inv_ready[p], before + 1)
                    eng.dma_start(r_dram[p].rearrange("b (j c) -> (b j) c", c=B * S // P), dc[p][:, :])\
                       .then_inc(inv_out[p], 16)
                    settled(eng, inv_out[p], before * 16 + 16)
                    spread_inverses(eng, p)
                    settled(eng, o_norm, h + 1)
                    for b in range(B):
                        eng.dma_start(o_dram[b][h],
                                      o_sb[p][32 * b:32 * b + HD, :]).then_inc(o_stored[p], 16)

                eng.wait_ge(first_in, 16 * 8)
                eng.sem_inc(head_in[0], 16 * QK_LOADS)
                for b in range(B - 2, B):
                    store_qk(eng, b, qk_out)
                eng.wait_ge(bg_ready, 1)
                eng.dma_start(bg_dram.rearrange("(o a) c -> o a c", o=1), bg_parts[:, :, :]).then_inc(bg_out, 16)
                eng.wait_ge(bg_out, 16)
                eng.dma_start(bg_rows[:, :], bg_dram).then_inc(bg_out, 16)
                eng.wait_ge(qk_out, 16 * 4 * B)
                eng.wait_ge(bg_out, 32)
                eng.wait_ge(filled, FILLS)
                eng.sem_inc(queue_steps, 1)
                with eng.Fori(0, NH2) as i:
                    settled(eng, groups_done, i * (2 * GPH) + SETS)
                    load(i * 2 + 1, 1)
                    with eng.If(i > 0):
                        settled(eng, o_ready[0], i * 2 + 1)
                        settled(eng, o_ready[1], i * 2 + 1)
                        normalise_and_store(i * 2 - 1, 1, i - 1)
                    settled(eng, groups_done, i * (2 * GPH) + (GPH + SETS))
                    with eng.If(i < NH2 - 1):
                        load(i * 2 + 2, 0)
                    settled(eng, o_ready[0], i * 2 + 2)
                    settled(eng, o_ready[1], i * 2 + 2)
                    normalise_and_store(i * 2, 0, i)

            @block.gpsimd
            def _(eng):
                for n, (dst, value) in enumerate(fills[1]):
                    eng.wait_ge(filled, FILLS0 + n)
                    eng.memset(dst, value).then_inc(filled, 1)
                eng.wait_ge(filled, FILLS)
                eng.sem_inc(queue_steps, 1)
                with eng.Fori(0, NH2) as i:
                    settled(eng, groups_done, i * (2 * GPH) + SETS)
                    copy_v(eng, in_range(i * 2 + 1), 1)
                    with eng.If(i > 0):
                        settled(eng, rd_in, i * (2 * 16 * B))
                        eng.tensor_tensor(o_sb[1], o_sb[1], rd[:, :], ALU.mult).then_inc(o_norm, 1)
                    settled(eng, groups_done, i * (2 * GPH) + (GPH + SETS))
                    with eng.If(i < NH2 - 1):
                        copy_v(eng, in_range(i * 2 + 2), 0)
                    settled(eng, rd_in, i * (2 * 16 * B) + 16 * B)
                    eng.tensor_tensor(o_sb[0], o_sb[0], rd[:, :], ALU.mult).then_inc(o_norm, 1)

            @block.tensor
            def _(eng):
                def scores(i, g, b):
                    p, t = (g // GPH) % 2, g % GPH
                    by_vector = b < DPG
                    if b == 0 and t == 0:
                        eng.wait_ge(head_in[p], (i + (g // (2 * GPH))) * (16 * LOADS) + 16 * LOADS)
                    if by_vector:
                        k = DPG * g + b
                        u = unit(k)
                        if k >= 2:
                            eng.wait_ge(z_ready, i * (2 * DPH) + (k - 1))
                    else:
                        u = 4
                        if g:
                            eng.wait_ge(p_ready, i * (8 * GPH) + 4 * g)
                    keys = slice(b * S + t * P, b * S + (t + 1) * P)
                    for c in range(2):
                        last = eng.matmul(ps[:, u + c, :], kb[p][:, keys],
                                          qb[p][:, b * S + c * HALF:b * S + (c + 1) * HALF],
                                          start=True, stop=True)
                    if by_vector:
                        last.then_inc(sd_ready, 1)
                        return
                    for c in range(2):
                        for m in range(2):
                            c0 = t * P + 64 * m + c * HALF
                            last = eng.matmul(ps[64 * m:64 * m + 64, u + c, :], ident2[:, :],
                                              t64[p][:, c0:c0 + HALF], start=False, stop=True,
                                              skip_group_check=True)
                    last.then_inc(sp_ready, 1)

                def products(i, g, c):
                    p, t = (g // GPH) % 2, g % GPH
                    if c == 0:
                        eng.wait_ge(p_ready, i * (8 * GPH) + 4 * (g + 1))
                        if t == 0:
                            eng.wait_ge(vst_in, i * 2 + (p + 1))
                    if t == 0:
                        eng.wait_ge(o_ready[c], i * 2 + (p + 1))
                    for b in range(B):
                        last = eng.matmul(ps[32 * b:32 * b + 32, 6 + c, :], vst[p][:, b * TB + t, :],
                                          slot(g, b)[:, c * HALF:(c + 1) * HALF],
                                          start=(t == 0), stop=(t == TB - 1))
                    if c == 1:
                        last.then_inc(groups_done, 1)
                    elif t == TB - 1:
                        last.then_inc(half_done, 1)

                for g in range(LAG):
                    for b in range(B):
                        scores(0, g, b)
                with eng.Fori(0, NH2) as i:
                    for g in range(2 * GPH):
                        for steps, c in (((0,), 0), ((1,), 1), ((2, 3), None)):
                            if g < 2 * GPH - LAG:
                                for b in steps:
                                    scores(i, g + LAG, b)
                            else:
                                with eng.If(i < NH2 - 1):
                                    for b in steps:
                                        scores(i, g + LAG, b)
                            if c is not None:
                                products(i, g, c)

            @block.vector
            def _(eng):
                def add_bias(i, g, b):
                    p, t, k = (g // GPH) % 2, g % GPH, DPG * g + b
                    eng.wait_ge(sd_ready, i * (2 * DPH) + (k + 1))
                    if b == 0:
                        eng.wait_ge(groups_done, i * (2 * GPH) + (g + 1))
                    eng.tensor_tensor(slot(g, b), banks(unit(k), 2), t128[p][:, t * P:t * P + S],
                                      ALU.add).then_inc(z_ready, 1)

                with eng.Fori(0, NH2) as i:
                    for g in range(2 * GPH):
                        if g == SETS // 2:
                            eng.wait_ge(qk_out, 16 * 4 * B)
                        for b in range(DPG):
                            add_bias(i, g, b)
                            if b == 0 and g == LAG - 1:
                                with eng.If(i > 0):
                                    eng.wait_ge(half_done, i * 2)
                                    eng.wait_ge(o_stored[1], i * (16 * B))
                                    copy_half(eng, 1, 0).then_inc(o_ready[0], 1)
                            if b == 0 and g == GPH + LAG - 1:
                                eng.wait_ge(half_done, i * 2 + 1)
                                eng.wait_ge(o_stored[0], i * (16 * B) + 16 * B)
                                copy_half(eng, 0, 0).then_inc(o_ready[0], 1)
                        if g == LAG + 1:
                            with eng.If(i > 0):
                                eng.wait_ge(den_in[1], i * 16)
                                eng.reciprocal(dc[1][:, :], dc[1][:, :]).then_inc(inv_ready[1], 1)
                        if g == GPH + LAG + 1:
                            eng.wait_ge(den_in[0], i * 16 + 16)
                            eng.reciprocal(dc[0][:, :], dc[0][:, :]).then_inc(inv_ready[0], 1)
                eng.wait_ge(half_done, H)
                eng.wait_ge(o_stored[1], NH2 * 16 * B)
                copy_half(eng, 1, 0).then_inc(o_ready[0], 1)

            @block.scalar
            def _(eng):
                with eng.Fori(0, NH2) as i:
                    for g in range(2 * GPH):
                        for b in range(B):
                            buf = slot(g, b)
                            if b < DPG:
                                eng.wait_ge(z_ready, i * (2 * DPH) + (DPG * g + b + 1))
                                eng.activation(buf, buf, ACT.Exp).then_inc(p_ready, 1)
                            else:
                                if g == SETS // 2:
                                    eng.wait_ge(qk_out, 16 * 4 * B)
                                eng.wait_ge(sp_ready, i * (2 * GPH) + (g + 1))
                                eng.wait_ge(groups_done, i * (2 * GPH) + (g + 1))
                                eng.activation(buf, banks(4, 2), ACT.Exp).then_inc(p_ready, 1)
                            if b == 0 and g == LAG - 1:
                                with eng.If(i > 0):
                                    eng.wait_ge(groups_done, i * (2 * GPH) + SETS)
                                    eng.wait_ge(o_stored[1], i * (16 * B))
                                    copy_half(eng, 1, 1).then_inc(o_ready[1], 1)
                            if b == 0 and g == GPH + LAG - 1:
                                eng.wait_ge(groups_done, i * (2 * GPH) + (GPH + SETS))
                                eng.wait_ge(o_stored[0], i * (16 * B) + 16 * B)
                                copy_half(eng, 0, 1).then_inc(o_ready[1], 1)
                eng.wait_ge(groups_done, H * GPH + SETS)
                eng.wait_ge(o_stored[1], NH2 * 16 * B)
                copy_half(eng, 1, 1).then_inc(o_ready[1], 1)

            num = [pbuf[:, b, :] for b in range(B)]
            PAIR = 2
            NP = NT // PAIR
            PB = NP // B
            gate = o_sbs[:, :, :].rearrange("p a (n c) -> p (a n) c", c=PAIR * D)
            NG = 8
            xn2 = splitf[:, 0:NTOK].rearrange("p (n d) -> p n d", d=D)
            xn2T = splitf[:, NTOK:2 * NTOK]
            expo = v_all[:, :, :].rearrange("p n d -> p (n d)")
            x8T = qb[0][:, :].bitcast(BF16)
            yb = kb[0][:, :].bitcast(BF16)
            w8T = sb("w8T", [P, D], BF16)
            wv = sb("wv", [P, D], F32)
            wexpo = sb("wexpo", [P, D], F32)
            amax = sb("amax", [P, B + 2], F32)
            srow = sb("srow", [1, 8], F32)
            scol = sb("scol", [P, 4], F32)
            NORM, TURN = 5, 7
            VT = 5

            num_in = [sem(f"num_in{b}") for b in range(B)]
            gated = sem("gated")
            sig_ready = sem("sig_ready")
            prod_ready = sem("prod_ready")
            x1_ready = sem("x1_ready")
            var2_ready = sem("var2_ready")
            rstd2_ready = sem("rstd2_ready")
            shift_ready = sem("shift_ready")
            xn2v_ready = sem("xn2v_ready")
            xn2s_ready = sem("xn2s_ready")
            xn2T_ps = sem("xn2T_ps")
            xn2T_ready = sem("xn2T_ready")
            amax_ready = sem("amax_ready")
            wT_ps = sem("wT_ps")
            amaxT_ps = sem("amaxT_ps")
            srow_ready = sem("srow_ready")
            scol_ps = sem("scol_ps")
            scol_ready = sem("scol_ready")
            wv_ready = sem("wv_ready")
            xs_ready = sem("xs_ready")
            expo_ready = sem("expo_ready")
            sum_ready = sem("sum_ready")
            sumv_ready = sem("sumv_ready")
            shift = sb("shift", [P, NT], F32)
            x8_ready = sem("x8_ready")
            w8_ready = sem("w8_ready")
            y_ps = sem("y_ps")
            y_ready = sem("y_ready")
            out_ready = sem("out_ready")
            outv_ready = sem("outv_ready")
            out_stored = sem("out_stored")
            out_t = out.rearrange("b (n p) d -> p (b n) d", p=P)
            HT = TB // 2
            half = [slice(NT - TB, NT - HT), slice(NT - HT, NT)]

            @block.sync
            def _(eng):
                def load_num(b):
                    eng.dma_start(num[b][0:P - HD, :], o_dram[b, 0:H - 1]).then_inc(num_in[b], 16)

                eng.wait_ge(o_ready[0], H + 1)
                eng.wait_ge(o_ready[1], H + 1)
                send_denominators(eng, 1)
                eng.wait_ge(o_stored[0], 16 * B * (NH2 + 1))
                eng.wait_ge(o_stored[1], 16 * B * NH2)
                load_num(0)
                eng.wait_ge(inv_ready[1], NH2)
                eng.dma_start(r_dram[1].rearrange("b (j c) -> (b j) c", c=B * S // P), dc[1][:, :])\
                   .then_inc(inv_out[1], 16)
                load_num(1)
                eng.wait_ge(inv_out[1], 16 * NH2)
                r = r_dram[1]
                eng.dma_start(rd[:, :], bass.AP(tensor=r.tensor, offset=r.offset, ap=[[S, B], [0, P // B], [1, S]]))\
                   .then_inc(rd_in, 16)
                load_num(2)
                load_num(3)
                eng.wait_ge(o_norm, H)
                for b in range(B):
                    eng.dma_start(num[b][P - HD:P, :], o_sb[1][32 * b:32 * b + HD, :]).then_inc(num_in[b], 16)
                for b in range(B - 1):
                    eng.wait_ge(out_ready, b + 1)
                    eng.dma_start(out_t[:, tiles(b), :], x_sb[:, tiles(b), :]).then_inc(out_stored, 16)
                eng.wait_ge(outv_ready, 1)
                eng.dma_start(out_t[:, half[1], :], x_sb[:, half[1], :]).then_inc(out_stored, 16)
                eng.wait_ge(out_ready, B)
                eng.dma_start(out_t[:, half[0], :], x_sb[:, half[0], :]).then_inc(out_stored, 16)
                eng.wait_ge(out_stored, 16 * (B + 1))

            @block.gpsimd
            def _(eng):
                def residual(j):
                    eng.wait_ge(prod_ready, j + 1)
                    xs = x_sb[:, PAIR * j:PAIR * (j + 1), :].rearrange("p n d -> p (n d)")
                    eng.tensor_tensor(xs, xs, gate[:, j % NG, :], ALU.add).then_inc(x1_ready, 1)

                def inverse_std(b):
                    eng.wait_ge(var2_ready, b + 1)
                    eng.tensor_scalar(st[:, 1, tiles(b)], mv[:, tiles(b), 1], EPS, None, ALU.add)\
                       .then_inc(rstd2_ready, 1)
                    eng.wait_ge(rstd2_ready, 2 * b + 1)
                    eng.tensor_tensor(st[:, 0, tiles(b)], st[:, 1, tiles(b)], minus_half[:, tiles(b)], ALU.pow)\
                       .then_inc(rstd2_ready, 1)

                for j in range(NP + 3):
                    if j < NP:
                        residual(j)
                    if j >= PB + 2 and (j - PB - 2) % PB == 0:
                        inverse_std((j - PB - 2) // PB)

                def round_up(b):
                    eng.wait_ge(expo_ready, b + 1)
                    eng.tensor_tensor(xn2T[:, cols(b)], xn2T[:, cols(b)], expo[:, cols(b)], ALU.add)\
                       .then_inc(sum_ready, 1)

                def last_residual(t, c, ready):
                    eng.wait_ge(y_ready, ready)
                    xs = x_sb[:, t, :].rearrange("p n d -> p (n d)")
                    eng.tensor_tensor(xs, xs, yb[:, c], ALU.add).then_inc(out_ready, 1)

                for b in range(1, B):
                    round_up(b)
                for b in range(B - 1):
                    last_residual(tiles(b), cols(b), b + 1)
                last_residual(half[0], slice(NTOK - S, NTOK - S + S // 2), B)

            @block.tensor
            def _(eng):
                eng.transpose(ps[:, 4, 0:P], wffn[:, :], ident[:, :]).then_inc(wT_ps, 1)

                def spread_maximum(col, bank, n):
                    eng.wait_ge(amax_ready, n + 1)
                    eng.transpose(ps[0:1, bank, 0:P], amax[:, col:col + 1], ident[:, :]).then_inc(amaxT_ps, 1)
                    eng.wait_ge(srow_ready, n + 1)
                    eng.matmul(ps[:, bank, 256:258], ones_row[:, :], srow[:, 2 * n:2 * n + 2],
                               start=True, stop=True).then_inc(scol_ps, 1)

                spread_maximum(B + 1, 5, 0)
                eng.wait_ge(o_ready[0], H + 1)
                eng.wait_ge(o_ready[1], H + 1)
                for _ in range(WARM_GATE):
                    eng.matmul(ps[:, 0, :], zeros[:, 0:P], zeros[:, :], start=True, stop=True)

                def gate_products(j):
                    if j == 0:
                        eng.wait_ge(num_in[0], 32)
                    if j == PB:
                        for b in range(1, B):
                            eng.wait_ge(num_in[b], 32)
                    if j >= 4:
                        eng.wait_ge(prod_ready, j - 3)
                    for m in range(PAIR):
                        n = PAIR * j + m
                        dst = ps[:, j % 4, m * 2 * D:(m + 1) * 2 * D]
                        eng.matmul(dst, num[n // TB][:, (n % TB) * P:(n % TB + 1) * P], wgate[:, :],
                                   start=True, stop=False)
                        last = eng.matmul(dst, bg_ones[:, :], bg_rows[:, :], start=False, stop=True)
                    last.then_inc(gated, 1)

                def turn(b):
                    eng.wait_ge(xn2v_ready, b + 1)
                    eng.wait_ge(xn2s_ready, b + 1)
                    if b == 0:
                        eng.wait_ge(wv_ready, 1)
                        eng.wait_ge(scol_ready, 1)
                    if b >= 2:
                        eng.wait_ge(xn2T_ready, b - 1)
                    for n in range(TB):
                        last = eng.transpose(banks(4 + 2 * (b % 2), 2)[:, n * P:(n + 1) * P],
                                             xn2[:, b * TB + n, :], ident[:, :])
                    last.then_inc(xn2T_ps, 1)

                for j in range(NP):
                    gate_products(j)
                    if j >= PB - 1 + TURN and (j - PB + 1 - TURN) % PB == 0:
                        turn((j - PB + 1 - TURN) // PB)
                turn(B - 2)
                turn(B - 1)
                eng.wait_ge(prod_ready, NP)
                spread_maximum(B, 0, 1)
                eng.wait_ge(w8_ready, 1)
                for b in range(B):
                    eng.wait_ge(x8_ready, b + 1)
                    if b == 0:
                        eng.wait_ge(xn2T_ready, B)
                    if b >= 2:
                        eng.wait_ge(y_ready, b - 1)
                    for n in range(TB):
                        last = eng.matmul(banks(2 * (b % 2) + 4, 2)[:, n * D:(n + 1) * D],
                                          x8T[:, b * S + n * P:b * S + (n + 1) * P], w8T[:, :],
                                          start=True, stop=True)
                    last.then_inc(y_ps, 1)

            @block.scalar
            def _(eng):
                eng.wait_ge(scol_ready, 1)
                eng.activation(wv[:, :], ps[:, 4, 0:P], ACT.Copy, scale=scol[:, 2:3]).then_inc(wv_ready, 1)

                def sigmoid(j):
                    eng.wait_ge(gated, j + 1)
                    if j >= NG:
                        eng.wait_ge(x1_ready, j - NG + 1)
                    eng.activation(gate[:, j % NG, :].rearrange("p (m d) -> p m d", d=D),
                                   ps[:, j % 4, :].rearrange("p (m c) -> p m c", c=2 * D)[:, :, D:2 * D],
                                   ACT.Sigmoid).then_inc(sig_ready, 1)

                def normalise(b):
                    eng.wait_ge(shift_ready, b + 1)
                    for n in range(b * TB + VT, (b + 1) * TB):
                        last = eng.activation(xn2[:, n, :], x_sb[:, n, :], ACT.Identity,
                                              bias=shift[:, n:n + 1], scale=st[:, 0, n:n + 1])
                    last.then_inc(xn2s_ready, 1)

                def turn(b):
                    eng.wait_ge(xn2T_ps, b + 1)
                    eng.activation(xn2T[:, cols(b)], banks(4 + 2 * (b % 2), 2), ACT.Copy).then_inc(xn2T_ready, 1)

                for j in range(NP):
                    sigmoid(j)
                    if j >= PB - 1 + NORM and (j - PB + 1 - NORM) % PB == 0:
                        normalise((j - PB + 1 - NORM) // PB)
                    if j >= PB - 1 + TURN + 1 and (j - PB - TURN) % PB == 0:
                        turn((j - PB - TURN) // PB)
                normalise(B - 2)
                turn(B - 2)
                normalise(B - 1)
                turn(B - 1)
                eng.wait_ge(scol_ready, 2)
                for b in range(B):
                    eng.wait_ge(xn2T_ready, b + 1)
                    eng.activation(xn2T[:, cols(b)], xn2T[:, cols(b)], ACT.Copy, scale=scol[:, 0:1])\
                       .then_inc(xs_ready, 1)

            @block.vector
            def _(eng):
                def scales(col, bank, n):
                    s = srow[:, 2 * n:2 * n + 2]
                    eng.wait_ge(amaxT_ps, n + 1)
                    chain(eng, eng.tensor_reduce(srow[:, 4:5], ps[0:1, bank, 0:P], AX.X, ALU.max))
                    chain(eng, eng.tensor_scalar(srow[:, 4:5], srow[:, 4:5], 1e-12, None, ALU.max))
                    chain(eng, eng.reciprocal(srow[:, 4:5], srow[:, 4:5]))
                    chain(eng, eng.tensor_scalar(s[:, 0:1], srow[:, 4:5], FP8_MAX, FP8_MAX, ALU.mult, ALU.min))
                    eng.reciprocal(s[:, 1:2], s[:, 0:1]).then_inc(srow_ready, 1)
                    eng.wait_ge(scol_ps, n + 1)
                    eng.tensor_copy(scol[:, 2 - 2 * n:4 - 2 * n], ps[:, bank, 256:258]).then_inc(scol_ready, 1)

                def exponents(v, c):
                    chain(eng, eng.tensor_scalar(c.bitcast(I32), v.bitcast(I32), 0x7F800000, None,
                                                 ALU.bitwise_and))
                    return eng.tensor_scalar(c, c, 2.0 ** -6, 1.5 * 2.0 ** 20, ALU.max, ALU.mult)

                def held(dst, done):
                    eng.tensor_scalar(dst, dst, FP8_MAX, -FP8_MAX, ALU.min, ALU.max).then_inc(done, 1)

                eng.tensor_reduce(amax[:, B + 1:B + 2], wffn[:, :], AX.X, ALU.max, apply_absolute_value=True)\
                   .then_inc(amax_ready, 1)
                scales(B + 1, 5, 0)
                eng.wait_ge(den_in[1], 16 * NH2)
                eng.reciprocal(dc[1][:, :], dc[1][:, :]).then_inc(inv_ready[1], 1)
                eng.wait_ge(wv_ready, 1)
                chain(eng, exponents(wv[:, :], wexpo[:, :]))
                chain(eng, eng.tensor_tensor(wv[:, :], wv[:, :], wexpo[:, :], ALU.add))
                chain(eng, eng.tensor_tensor(w8T[:, :], wv[:, :], wexpo[:, :], ALU.subtract))
                held(w8T[:, :], w8_ready)
                eng.wait_ge(rd_in, 16 * B * (H - 1) + 16)
                eng.tensor_tensor(o_sb[1], o_sb[1], rd[:, :], ALU.mult).then_inc(o_norm, 1)

                def product(j):
                    eng.wait_ge(sig_ready, j + 1)
                    eng.tensor_tensor(gate[:, j % NG, :].rearrange("p (m d) -> p m d", d=D),
                                      ps[:, j % 4, :].rearrange("p (m c) -> p m c", c=2 * D)[:, :, 0:D],
                                      gate[:, j % NG, :].rearrange("p (m d) -> p m d", d=D),
                                      ALU.mult).then_inc(prod_ready, 1)

                def stats_of(j):
                    eng.wait_ge(x1_ready, j + 1)
                    for n in range(PAIR * j, PAIR * (j + 1)):
                        last = eng.bn_stats(stats[:, n, :], x_sb[:, n, :])
                    if (j + 1) % PB == 0:
                        chain(eng, last)
                        for n in range((j + 1) * PAIR - TB, (j + 1) * PAIR):
                            last = eng.bn_aggr(mv[:, n, :], stats[:, n, :])
                        last.then_inc(var2_ready, 1)

                def normalise(b):
                    eng.wait_ge(rstd2_ready, 2 * b + 2)
                    eng.scalar_tensor_tensor(out=shift[:, tiles(b)], in0=mv[:, tiles(b), 0], scalar=-1.0,
                                             in1=st[:, 0, tiles(b)], op0=ALU.mult, op1=ALU.mult)\
                       .then_inc(shift_ready, 1)
                    for n in range(b * TB, b * TB + VT):
                        last = eng.tensor_scalar(xn2[:, n, :], x_sb[:, n, :], mv[:, n, 0:1],
                                                 st[:, 0, n:n + 1], ALU.subtract, ALU.mult)
                    last.then_inc(xn2v_ready, 1)

                def largest(b):
                    eng.wait_ge(xn2v_ready, b + 1)
                    eng.wait_ge(xn2s_ready, b + 1)
                    return eng.tensor_reduce(amax[:, b:b + 1], xn2[:, tiles(b), :], AX.XY, ALU.max,
                                             apply_absolute_value=True)

                for j in range(NP + 2):
                    if j < NP:
                        product(j)
                    if 2 <= j < NP + 2:
                        stats_of(j - 2)
                    if j >= PB - 1 + NORM and (j - PB + 1 - NORM) % PB == 0:
                        normalise((j - PB + 1 - NORM) // PB)
                    if PB + 1 + NORM <= j < NP + 2 and (j - PB - 1 - NORM) % PB == 0:
                        largest((j - PB - 1 - NORM) // PB)
                largest(B - 2)
                normalise(B - 1)
                chain(eng, largest(B - 1))
                eng.tensor_reduce(amax[:, B:B + 1], amax[:, 0:B], AX.X, ALU.max).then_inc(amax_ready, 1)
                scales(B, 0, 1)
                eng.wait_ge(scol_ready, 2)
                chain(eng, eng.tensor_tensor(scol[:, 3:4], scol[:, 3:4], scol[:, 1:2], ALU.mult))

                def exponents_of(b):
                    eng.wait_ge(xs_ready, b + 1)
                    exponents(xn2T[:, cols(b)], expo[:, cols(b)]).then_inc(expo_ready, 1)

                def round_up(b):
                    eng.wait_ge(expo_ready, b + 1)
                    eng.tensor_tensor(xn2T[:, cols(b)], xn2T[:, cols(b)], expo[:, cols(b)], ALU.add)\
                       .then_inc(sumv_ready, 1)

                def round_down(b, summed, n):
                    eng.wait_ge(summed, n)
                    chain(eng, eng.tensor_tensor(x8T[:, cols(b)], xn2T[:, cols(b)], expo[:, cols(b)], ALU.subtract))
                    held(x8T[:, cols(b)], x8_ready)

                def finish(b, h=None):
                    n = TB if h is None else HT
                    n0 = 0 if h is None else h * HT
                    eng.wait_ge(y_ps, b + 1)
                    return eng.scalar_tensor_tensor(
                        out=yb[:, b * S + n0 * D:b * S + (n0 + n) * D].rearrange("p (n d) -> p n d", d=D),
                        in0=banks(2 * (b % 2) + 4, 2)[:, n0 * D:(n0 + n) * D].rearrange("p (n d) -> p n d", d=D),
                        scalar=scol[:, 3:4],
                        in1=bass.AP(tensor=ffn_bias[:, :].tensor, offset=ffn_bias[:, :].offset,
                                    ap=[list(ffn_bias[:, :].ap[0]), [0, n], [1, D]]),
                        op0=ALU.mult, op1=ALU.add)

                exponents_of(0)
                round_up(0)
                exponents_of(1)
                round_down(0, sumv_ready, 1)
                exponents_of(2)
                exponents_of(3)
                round_down(1, sum_ready, 1)
                finish(0).then_inc(y_ready, 1)
                round_down(2, sum_ready, 2)
                finish(1).then_inc(y_ready, 1)
                round_down(3, sum_ready, 3)
                finish(2).then_inc(y_ready, 1)
                finish(3, 0).then_inc(y_ready, 1)
                chain(eng, finish(3, 1))
                xs = x_sb[:, half[1], :].rearrange("p n d -> p (n d)")
                eng.tensor_tensor(xs, xs, yb[:, NTOK - S // 2:NTOK], ALU.add).then_inc(outv_ready, 1)


_INS = {"L0_attn_x": "x", "L0_attn_w_in": "w_in", "L0_attn_w_gate": "w_gate", "L0_attn_b_gate": "b_gate",
        "L0_attn_amplitudes": "amplitudes", "L0_attn_sharpness": "sharpness", "L0_attn_offsets": "offsets",
        "L0_ffn_weight": "w_ffn", "L0_ffn_bias": "ffn_bias"}


def kernel(**inputs):
    import numpy as np
    import concourse.bacc as bacc
    from concourse.bass_utils import run_bass_kernel_spmd

    pair = np.arange(PAIRS).reshape(PG, PP).T // KB
    consts = {
        "c_ident": np.eye(P, dtype=np.float32),
        "c_ident2": np.concatenate([np.eye(64), np.eye(64)]).astype(np.float16),
        "c_sel": (pair[:, :, None] == np.arange(32)).astype(np.float32),
        "c_hsel": (np.arange(P)[:, None] // HD == np.arange(32)).astype(np.float32),
        "c_rel": (np.arange(GN) - (S - 1)).astype(np.float32),
    }
    nc = bacc.Bacc("TRN2", target_bir_lowering=False, num_devices=1)
    arrays = {f"in_{name}": np.ascontiguousarray(inputs[name]) for name in _INS}
    arrays.update(consts)
    io = {}
    for name, a in arrays.items():
        short = _INS[name[3:]] if name[3:] in _INS else name
        io[short] = nc.dram_tensor(name, a.shape, mybir.dt.from_np(a.dtype), kind="ExternalInput").ap()
    out = nc.dram_tensor("out_0", (B, S, D), F32, kind="ExternalOutput").ap()
    attention_block(nc, io, out)
    r = run_bass_kernel_spmd(nc, [arrays], core_ids=[0])
    return r.results[0]["out_0"]
```
